# Optimizing a Trainium2 kernel written in Bass

```python
import numpy as np
import jax
import jax.numpy as jnp

def _softmax(x, axis=-1):
    return jax.nn.softmax(x, axis=axis)

def _gelu(x):
    return jax.nn.gelu(x, approximate=True)

def _silu(x):
    return jax.nn.silu(x)

def _sigmoid(x):
    return jax.nn.sigmoid(x)

def _layernorm(x, axis=-1, eps=1e-05):
    m = jnp.mean(x, axis=axis, keepdims=True)
    v = jnp.var(x, axis=axis, keepdims=True)
    return (x - m) / jnp.sqrt(v + eps)

def _scatter_add(tgt, idx, src, axis=0):
    return tgt.at[idx].add(src)

def _segment_sum(src, seg, n):
    return jax.ops.segment_sum(src, seg, n)
kernel_name = 'mk_gnn_preln_d1_gnn_r8_6d8190'

def setup_inputs(seed: int=0):
    np.random.seed(seed)
    _w = jnp.asarray

    def _rec_inputs():
        import jax
        import jax.numpy as jnp
        _gk = jax.random.key(seed)
        x = -0.0006008 + 1.001 * jax.random.normal(jax.random.fold_in(_gk, 1), (6250, 256), jnp.float32)
        _s = jax.random.randint(jax.random.fold_in(_gk, 2), (50000,), 0, 6250, jnp.int32)
        _d = jax.random.randint(jax.random.fold_in(_gk, 3), (50000,), 0, 6250, jnp.int32)
        _loop = jnp.arange(6250, dtype=jnp.int32)
        src = jnp.concatenate([_s, _d, _loop])
        dst = jnp.concatenate([_d, _s, _loop])
        _o = jnp.argsort(dst, stable=True)
        src = src[_o]
        dst = dst[_o]
        edge_attr_256 = -0.000128692 + 0.999872 * jax.random.normal(jax.random.fold_in(_gk, 12), (106250, 256), jnp.float32)
        return (x, src, dst, edge_attr_256)
    x, src, dst, edge_attr_256 = _rec_inputs()

    def _L0_gnn_setup():
        import jax, jax.numpy as jnp
        import numpy as np
        N_NODES = 1250
        N_EDGES = 20000
        D_IN = 256
        D_EDGE = 256
        D_HID = 256
        D_OUT = 256
        key = jax.random.key(seed)
        ks = jax.random.split(key, 12)
        s = 1.0 / np.sqrt(D_IN)
        se = 1.0 / np.sqrt(D_EDGE)
        sh = 1.0 / np.sqrt(D_HID)
        return {'nfeat': jax.random.normal(ks[0], (N_NODES, D_IN), dtype=jnp.float32), 'efeat': jax.random.normal(ks[1], (N_EDGES, D_EDGE), dtype=jnp.float32), 'src': jax.random.randint(ks[2], (N_EDGES,), 0, N_NODES, dtype=jnp.int32), 'dst': jax.random.randint(ks[3], (N_EDGES,), 0, N_NODES, dtype=jnp.int32), 'Wq': jax.random.uniform(ks[4], (D_IN, D_HID), jnp.float32, -s, s), 'bq': jax.random.uniform(ks[5], (D_HID,), jnp.float32, -s, s), 'Wk': jax.random.uniform(ks[6], (D_IN, D_HID), jnp.float32, -s, s), 'bk': jax.random.uniform(ks[7], (D_HID,), jnp.float32, -s, s), 'We': jax.random.uniform(ks[8], (D_EDGE, D_HID), jnp.float32, -se, se), 'be': jax.random.uniform(ks[9], (D_HID,), jnp.float32, -se, se), 'Wr': jax.random.uniform(ks[10], (D_HID, D_OUT), jnp.float32, -sh, sh), 'br': jax.random.uniform(ks[11], (D_OUT,), jnp.float32, -sh, sh)}
    _L0_gnn_all = _L0_gnn_setup()
    _L0_gnn_in = {k: v for k, v in _L0_gnn_all.items() if k in ('Wq', 'bq', 'Wk', 'bk', 'We', 'be', 'Wr', 'br')}
    del _L0_gnn_all
    return {'x': x, 'src': src, 'dst': dst, 'edge_attr_256': edge_attr_256, 'L0_gnn_Wq': _L0_gnn_in['Wq'], 'L0_gnn_bq': _L0_gnn_in['bq'], 'L0_gnn_Wk': _L0_gnn_in['Wk'], 'L0_gnn_bk': _L0_gnn_in['bk'], 'L0_gnn_We': _L0_gnn_in['We'], 'L0_gnn_be': _L0_gnn_in['be'], 'L0_gnn_Wr': _L0_gnn_in['Wr'], 'L0_gnn_br': _L0_gnn_in['br']}

def reference(x, src, dst, edge_attr_256, L0_gnn_Wq, L0_gnn_bq, L0_gnn_Wk, L0_gnn_bk, L0_gnn_We, L0_gnn_be, L0_gnn_Wr, L0_gnn_br):
    import jax
    import jax.numpy as jnp

    def _L0_gnn_ref(nfeat, efeat, src, dst, Wq, bq, Wk, bk, We, be, Wr, br):
        import jax, jax.numpy as jnp
        import numpy as np
        N_NODES = 1250
        N_EDGES = 20000
        D_IN = 256
        D_EDGE = 256
        D_HID = 256
        D_OUT = 256
        n_nodes = nfeat.shape[0]
        eq = nfeat @ Wq + bq
        ek = nfeat @ Wk + bk
        e = efeat @ We + be
        m = jax.nn.relu(eq[dst] + ek[src] + e)
        ft = jax.ops.segment_sum(m, dst, num_segments=n_nodes)
        return ft @ Wr + br
    h = jnp.maximum(_layernorm(x, axis=-1), 0.0)
    x = x + _L0_gnn_ref(h, edge_attr_256, src, dst, L0_gnn_Wq, L0_gnn_bq, L0_gnn_Wk, L0_gnn_bk, L0_gnn_We, L0_gnn_be, L0_gnn_Wr, L0_gnn_br)
    return x

_drawn_inputs = setup_inputs


def setup_inputs(seed=0):
    import zlib

    import numpy as np

    out = dict(_drawn_inputs(seed))
    spreads = {}
    factors = {'L0_gnn_br': 6.673}
    for name, (base, spread) in spreads.items():
        noise = np.random.default_rng([zlib.crc32(name.encode()), seed]).standard_normal(out[name].shape)
        drawn = base * np.exp(spread * noise) if base else spread * noise
        out[name] = jnp.asarray(drawn.astype(out[name].dtype))
    for name, factor in factors.items():
        out[name] = (out[name] * factor).astype(out[name].dtype)
    return out
```

```python
import numpy as np
import concourse.bass as bass
from concourse import mybir
from contextlib import ExitStack

LANES = 128
NODES = 6250
EDGES = 106250
D = 256
HALVES = D // LANES
BLOCKS = 50
ROWS = BLOCKS * LANES
TILES = 4
GROUP = TILES * LANES
GROUPS = -(-EDGES // GROUP)
UNROLL = 4
BODIES = GROUPS // UNROLL
CHUNKS = 2
GPART = GROUPS // CHUNKS
WIN = 48
PASSES = -(-NODES // WIN)
NO_NODE = -1
FAR = 1 << 20
EPS = 1e-5
XPARTS = 5
XPART = BLOCKS // XPARTS
NRING = 2
assert GROUPS % UNROLL == 0 and GROUPS % CHUNKS == 0 and PASSES * WIN <= ROWS


def gnn_program(nc, x, dst_groups, dst_lanes, src_lanes, edges, Wq, bq, Wk, bk, We, be, Wr, br, out):
    F32, F32R = mybir.dt.float32, mybir.dt.float32r
    I32, I16 = mybir.dt.int32, mybir.dt.int16
    ALU, ACT, AX = mybir.AluOpType, mybir.ActivationFunctionType, mybir.AxisListType

    k_table = nc.dram_tensor("k_table", (ROWS, D), F32, kind="Internal").ap()
    q_table = nc.dram_tensor("q_table", (2, ROWS, D), F32R, kind="Internal").ap()
    rel_table = nc.dram_tensor("rel_table", (GROUPS, GROUP), I16, kind="Internal").ap()
    range_table = nc.dram_tensor("range_table", (2, GROUPS), F32, kind="Internal").ap()

    x_blocks = x.rearrange("(b p) d -> b p d", p=LANES)
    out_blocks = out.rearrange("(b p) d -> b p d", p=LANES)
    k_blocks = k_table.rearrange("(b p) d -> b p d", p=LANES)
    q_blocks = q_table.rearrange("s (b p) d -> s b p d", p=LANES)

    ctx = ExitStack()
    with ctx:
        def sb(name, shape, dt):
            return ctx.enter_context(nc.sbuf_tensor(name, shape, dt))

        def pb(name, shape):
            return ctx.enter_context(nc.psum_tensor(name, shape, F32))

        def sem(name):
            return ctx.enter_context(nc.semaphore(name))

        ident = sb("ident", [LANES, LANES], F32)
        window_cols = sb("window_cols", [LANES, PASSES * WIN], I16)
        lane_raw = sb("lane_raw", [2 * WIN, PASSES], F32)
        lane_wrap = sb("lane_wrap", [2 * WIN, 1], F32)
        lane_node = sb("lane_node", [2 * WIN, PASSES], F32)
        lane_id = sb("lane_id", [2 * WIN, 1], F32)
        src_idx = sb("src_idx", [LANES, GROUPS, TILES], I32)
        dst_idx = sb("dst_idx", [LANES, GROUPS, TILES], I32)
        rel_idx = sb("rel_idx", [LANES, GROUPS, TILES], F32)
        rel_g = sb("rel_g", [GPART, CHUNKS, GROUP], I16)
        top_g = sb("top_g", [GPART, CHUNKS], F32)
        low_g = sb("low_g", [GPART, CHUNKS], F32)
        win_g = sb("win_g", [GPART, CHUNKS], F32)
        ranges = sb("ranges", [LANES, 2, GROUPS], F32)
        spans = sb("spans", [LANES, GROUPS], F32)
        span = sb("span", [LANES, 1], F32)
        narrow = sb("narrow", [LANES, 1], F32)
        win_f = sb("win_f", [LANES, GROUPS], F32)
        win_tab = sb("win_tab", [LANES, GROUPS], I32)
        more_passes = sb("more_passes", [LANES, 1], I32)

        w_hi = sb("w_hi", [LANES, HALVES, 2 * D], F32R)
        w_lo = sb("w_lo", [LANES, HALVES, 2 * D], F32R)
        we_hi = sb("we_hi", [LANES, HALVES, D], F32R)
        we_lo = sb("we_lo", [LANES, HALVES, D], F32R)
        wr_hi = sb("wr_hi", [LANES, HALVES, D], F32R)
        wr_lo = sb("wr_lo", [LANES, HALVES, D], F32R)
        bias = sb("bias", [LANES, 2 * D], F32)
        bias_e = sb("bias_e", [LANES, D], F32)
        bias_r = sb("bias_r", [LANES, D], F32)

        stats = sb("stats", [LANES, BLOCKS, 6], F32)
        norm = sb("norm", [LANES, 6, BLOCKS], F32)
        mean2, diff, var, root, rstd, shift = (norm[:, i, :] for i in range(6))
        hn = sb("hn", [LANES, NRING, D], F32)
        hT_hi = sb("hT_hi", [LANES, NRING, D], F32R)
        hT_lo = sb("hT_lo", [LANES, NRING, D], F32R)
        kq = sb("kq", [LANES, NRING, 2 * D], F32)
        q_hi = sb("q_hi", [LANES, NRING, D], F32R)
        q_lo = sb("q_lo", [LANES, NRING, D], F32R)

        ft = sb("ft", [LANES, HALVES, ROWS], F32)
        edge = sb("edge", [LANES, 4, HALVES, GROUP], F32)
        edge_hi = sb("edge_hi", [LANES, 2, HALVES, GROUP], F32R)
        edge_lo = sb("edge_lo", [LANES, 2, HALVES, GROUP], F32R)
        k_rows = sb("k_rows", [LANES, 4, TILES, D], F32)
        idx = sb("idx", [LANES, 4, TILES], I32)
        q_win = sb("q_win", [2 * WIN, 4, D], F32R)
        rel_row = sb("rel_row", [2 * WIN, 4, GROUP], I16)
        pick = sb("pick", [2 * WIN, 2, GROUP], F32R)
        send = sb("send", [LANES, 2, TILES, LANES], F32R)
        pre = sb("pre", [LANES, 2, TILES * D], F32)
        m_hi = sb("m_hi", [LANES, 2, TILES * D], F32R)
        m_lo = sb("m_lo", [LANES, 2, TILES * D], F32R)
        x_all = ft[:].rearrange("p h r -> p (h r)").rearrange("p (b d) -> p b d", d=D)
        xo = k_rows[:, 3, 0:NRING]
        dst_g = pre[0:GPART, 0, :].bitcast(I32).rearrange("p (c e) -> p c e", c=CHUNKS)
        dst_f = pre[0:GPART, 1, :].rearrange("p (c e) -> p c e", c=CHUNKS)
        w_raw = k_rows[:, 0].rearrange("p t d -> p (t d)").rearrange("p (h n) -> p h n", h=HALVES)
        we_raw = k_rows[:, 1, 0:HALVES]
        wr_raw = k_rows[:, 2, 0:HALVES]
        part = sb("part", [LANES, 2, D], F32)

        p_edge = pb("p_edge", [LANES, 2, TILES * D])
        p_sum = pb("p_sum", [LANES, 2, 512])
        p_turn = pb("p_turn", [LANES, 2, 512])

        s_dst = sem("dst_loaded")
        s_lanes = sem("lanes_loaded")
        s_wload = sem("weights_loaded")
        s_range = sem("range_stored")
        s_ranges = sem("ranges_loaded")
        s_rel = sem("rel_stored")
        s_prep = sem("prep_step")
        s_tab = sem("window_table_ready")
        s_wsplit = sem("weights_split")
        s_zero = sem("zeroed")
        s_const = sem("constants_ready")
        s_x = [sem(f"x_loaded_{c}") for c in range(XPARTS)]
        s_norm = sem("layernorm_step")
        s_var = sem("variance_ready")
        s_root = sem("deviation_ready")
        s_shift = sem("scale_and_shift_ready")
        s_stats = sem("row_statistics_ready")
        s_cleared = sem("ft_cleared")
        s_hn = sem("hn_ready")
        s_hT = sem("h_transposed")
        s_hhi = sem("hT_hi_ready")
        s_hlo = sem("hT_lo_ready")
        s_kqp = sem("kq_product_done")
        s_kq = sem("kq_ready")
        s_qhi = sem("q_hi_ready")
        s_qlo = sem("q_lo_ready")
        s_store = [sem(f"tables_stored_{u}") for u in range(NRING)]
        s_edge = [sem(f"edge_loaded_{u}") for u in range(UNROLL)]
        s_row = [sem(f"rel_row_loaded_{u}") for u in range(UNROLL)]
        s_win = [sem(f"q_window_loaded_{u}") for u in range(UNROLL)]
        s_rows = [sem(f"k_rows_gathered_{u}") for u in range(UNROLL)]
        s_go = sem("gathers_may_start")
        s_idx = sem("idx_ready")
        s_ehi = sem("edge_hi_ready")
        s_elo = sem("edge_lo_ready")
        s_pick = sem("pick_ready")
        s_send = sem("send_ready")
        s_prod = sem("edge_product_done")
        s_pre = sem("pre_ready")
        s_mhi = sem("m_hi_ready")
        s_mlo = sem("m_lo_ready")
        s_sum = sem("sum_done")
        s_part = sem("part_ready")
        s_turn = sem("part_transposed")
        s_ft = sem("ft_added")
        s_xo = [sem(f"xo_loaded_{u}") for u in range(NRING)]
        s_fhi = sem("ft_hi_ready")
        s_flo = sem("ft_lo_ready")
        s_outp = sem("out_product_done")
        s_xbr = sem("x_plus_br_ready")
        s_fin = sem("out_ready")
        s_out = [sem(f"out_stored_{u}") for u in range(NRING)]

        def after(eng, semaphore, n):
            if isinstance(n, int) and n < 0:
                return
            eng.wait_ge(semaphore, n + 1)

        def stored(eng, b, u):
            if isinstance(b, int) and b < NRING:
                return
            eng.wait_ge(s_store[u], 3 * 16 // NRING * (b - u))

        def visit(it, u):
            body, slot = it + u // UNROLL, u % UNROLL
            return body, slot, body * UNROLL + slot, body // BODIES, body % BODIES

        def window_start(eng, w, ps):
            return nc.s_assert_within(eng.snap(w + ps * WIN), 0, ROWS - WIN, skip_runtime_bounds_check_because=(
                "either there is one pass, or the window table is all zeros"))

        def passes_of(eng):
            eng.wait_ge(s_tab, 1)
            return eng.value_load(more_passes[0:1, 0:1], min_val=0, max_val=PASSES - 1) * BODIES + BODIES

        block = ctx.enter_context(nc.Block())

        @block.sync
        def _(sp):
            sp.dma_start(dst_g[:], dst_groups.rearrange("(p c) e -> p c e", c=CHUNKS)).then_inc(s_dst, 16)

            for c in range(XPARTS):
                blocks = slice(c * XPART, (c + 1) * XPART)
                sp.dma_start(x_all[:, blocks, :], x_blocks[blocks].rearrange("b p d -> p b d")).then_inc(s_x[c], 16)
            for w_ap, dst in ((Wk, w_raw[:, :, 0:D]), (Wq, w_raw[:, :, D:2 * D])):
                sp.dma_start(dst, w_ap.rearrange("(h p) n -> p h n", p=LANES)).then_inc(s_wload, 16)
            sp.dma_start(we_raw[:], We.rearrange("(h p) n -> p h n", p=LANES)).then_inc(s_wload, 16)
            sp.dma_start(wr_raw[:], Wr.rearrange("(h p) n -> p h n", p=LANES)).then_inc(s_wload, 16)
            for b_ap, dst in ((bk, bias[:, 0:D]), (bq, bias[:, D:2 * D]), (be, bias_e[:]), (br, bias_r[:])):
                sp.dma_start(dst, b_ap.rearrange("(a n) -> a n", a=1).to_broadcast([LANES, D]))\
                    .then_inc(s_wload, 16)
            sp.dma_start(dst_idx[:], dst_lanes).then_inc(s_lanes, 16)
            sp.dma_start(src_idx[:], src_lanes).then_inc(s_lanes, 16)
            sp.wait_ge(s_prep, 4)
            sp.dma_start(range_table[0].rearrange("(p c) -> p c", c=CHUNKS), low_g[:]).then_inc(s_range, 16)
            sp.dma_start(range_table[1].rearrange("(p c) -> p c", c=CHUNKS), top_g[:]).then_inc(s_range, 16)
            sp.wait_ge(s_range, 32)
            sp.dma_start(ranges[:], range_table.unsqueeze(0).to_broadcast([LANES, 2, GROUPS]))\
                .then_inc(s_ranges, 16)

            def store_tables(b, u):
                after(sp, s_kq, b)
                after(sp, s_qhi, b)
                after(sp, s_qlo, b)

                def at(t):
                    return t[b] if isinstance(b, int) else t[bass.ds(b, 1)].rearrange("a p d -> (a p) d")
                sp.dma_start(at(k_blocks), kq[:, u, 0:D]).then_inc(s_store[u], 16)
                sp.dma_start(at(q_blocks[0]).bitcast(F32), q_hi[:, u, :].bitcast(F32)).then_inc(s_store[u], 16)
                sp.dma_start(at(q_blocks[1]).bitcast(F32), q_lo[:, u, :].bitcast(F32)).then_inc(s_store[u], 16)

            def load_edge(it, u):
                body, slot, n, _, gb = visit(it, u)
                after(sp, s_ehi, n - 4)
                after(sp, s_elo, n - 4)
                g = gb * UNROLL + slot
                src = edges[g] if isinstance(g, int) else edges[bass.ds(g, 1)].rearrange("a p h e -> (a p) h e")
                sp.dma_start(edge[:, slot], src).then_inc(s_edge[slot], 16)

            for u in range(UNROLL):
                load_edge(0, u)
            sp.wait_ge(s_prep, 13)
            sp.dma_start(rel_table.rearrange("(p c) e -> p c e", c=CHUNKS), rel_g[:]).then_inc(s_rel, 16)
            with sp.Fori(0, BLOCKS // NRING) as it:
                for u in range(NRING):
                    store_tables(NRING * it + u, u)

            def load_row(it, u):
                body, slot, n, _, gb = visit(it, u)
                after(sp, s_pick, n - 4)
                g = gb * UNROLL + slot
                sp.dma_start(rel_row[:, slot, :], rel_table[bass.ds(g, 1), :].to_broadcast([2 * WIN, GROUP]))\
                    .then_inc(s_row[slot], 16)

            def load_window(it, u):
                body, slot, n, ps, gb = visit(it, u)
                g = gb * UNROLL + slot
                w = sp.value_load(win_tab[0:1, bass.ds(g, 1)], min_val=0, max_val=NODES - WIN)
                w0 = window_start(sp, w, ps)
                after(sp, s_prod, n - 4)
                for s in range(2):
                    sp.dma_start(q_win[s * WIN:(s + 1) * WIN, slot, :].bitcast(F32),
                                 q_table[s, bass.ds(w0, WIN), :].bitcast(F32)).then_inc(s_win[slot], 16)

            sp.wait_ge(s_rel, 16)
            for u in range(UNROLL):
                load_row(0, u)
            bodies = passes_of(sp)
            for u in range(NRING):
                sp.wait_ge(s_store[u], 16 * 3 * (BLOCKS // NRING))
            for u in range(UNROLL):
                load_window(0, u)
            with sp.Fori(1, bodies) as it:
                for u in range(UNROLL):
                    load_edge(it, u)
                    load_row(it, u)
                    load_window(it, u)

            def load_xo(b, u):
                after(sp, s_xbr, b - NRING)
                src = x_blocks[b] if isinstance(b, int) else x_blocks[bass.ds(b, 1)].rearrange("a p d -> (a p) d")
                sp.dma_start(xo[:, u, :], src).then_inc(s_xo[u], 16)

            def store_out(b, u):
                after(sp, s_fin, b)
                dst = out_blocks[b] if isinstance(b, int) else out_blocks[bass.ds(b, 1)].rearrange("a p d -> (a p) d")
                sp.dma_start(dst, hn[:, u, :]).then_inc(s_out[u], 16)

            sp.wait_ge(s_pre, bodies * UNROLL)
            load_xo(0, 0)
            load_xo(1, 1)
            with sp.Fori(0, BLOCKS // NRING - 1) as it:
                for u in range(NRING):
                    load_xo(NRING * it + NRING + u, u)
                    store_out(NRING * it + u, u)
            for b in range(BLOCKS - NRING, BLOCKS):
                store_out(b, b % NRING)
            for u in range(NRING):
                sp.wait_ge(s_out[u], 16 * (BLOCKS // NRING))

        @block.gpsimd
        def _(pool):
            nc.gpsimd.memset(ident[:], 0.0).then_inc(s_zero, 1)
            nc.gpsimd.iota(lane_raw[:], pattern=[[WIN, PASSES]], base=0, channel_multiplier=1,
                           allow_small_or_imprecise_dtypes=True).then_inc(s_const, 1)
            nc.gpsimd.iota(lane_id[:], pattern=[[0, 1]], base=0, channel_multiplier=1,
                           allow_small_or_imprecise_dtypes=True).then_inc(s_const, 1)
            pool.wait_ge(s_zero, 1)
            nc.gpsimd.affine_select(out=ident[:], in_=ident[:], compare_op=ALU.not_equal, fill=1.0, base=0,
                                    pattern=[[-1, LANES]], channel_multiplier=1).then_inc(s_const, 1)
            nc.gpsimd.iota(window_cols[:], pattern=[[1, PASSES * WIN]], base=0, channel_multiplier=0,
                           allow_small_or_imprecise_dtypes=True).then_inc(s_const, 1)
            nc.gpsimd.memset(send[:].bitcast(F32), 0.0).then_inc(s_const, 1)

            def make_q_lo(b, u):
                after(pool, s_qhi, b)
                stored(pool, b, u)
                nc.gpsimd.tensor_tensor(q_lo[:, u, :], kq[:, u, D:2 * D], q_hi[:, u, :].bitcast(F32),
                                        ALU.subtract).then_inc(s_qlo, 1)

            for b in range(NRING):
                make_q_lo(b, b)
            with pool.Fori(1, BLOCKS // NRING) as it:
                for u in range(NRING):
                    make_q_lo(NRING * it + u, u)

            bodies = passes_of(pool)
            for u in range(NRING):
                pool.wait_ge(s_store[u], 48 * (BLOCKS // NRING))

            def gather(it, u):
                _, slot, n, _, _ = visit(it, u)
                after(pool, s_idx, n)
                after(pool, s_pre, n - 4)
                pool.sem_inc(s_go, 1)
                for j in range(TILES):
                    nc.gpsimd.indirect_dma_start(
                        out=k_rows[:, slot, j, :], out_offset=None, in_=k_table,
                        in_offset=bass.IndirectOffsetOnAxis(ap=idx[:, slot, j:j + 1], axis=0),
                    ).then_inc(s_rows[slot], 16)

            for u in range(UNROLL):
                gather(0, u)
            with pool.Fori(1, bodies) as it:
                for u in range(UNROLL):
                    gather(it, u)

            def add_br(b, u):
                pool.wait_ge(s_xo[u], 16 // NRING * (b - u) + 16)
                after(pool, s_fin, b - NRING)
                nc.gpsimd.tensor_tensor(kq[:, u, 0:D], xo[:, u, :], bias_r[:], ALU.add).then_inc(s_xbr, 1)

            for b in range(NRING):
                add_br(b, b)
            with pool.Fori(1, BLOCKS // NRING) as it:
                for u in range(NRING):
                    add_br(NRING * it + u, u)

        @block.scalar
        def _(act):
            act.wait_ge(s_wload, 16 * 8)
            nc.scalar.activation(w_hi[:], w_raw[:], ACT.Copy).then_inc(s_wsplit, 1)
            nc.scalar.activation(we_hi[:], we_raw[:], ACT.Copy).then_inc(s_wsplit, 1)
            nc.scalar.activation(wr_hi[:], wr_raw[:], ACT.Copy).then_inc(s_wsplit, 1)

            act.wait_ge(s_var, 1)
            nc.scalar.activation(root, var, ACT.Sqrt).then_inc(s_root, 1)
            act.wait_ge(s_shift, 1)

            def make_h(b, u):
                after(act, s_hT, b - NRING)
                nc.scalar.activation(hn[:, u, :], x_all[:, bass.ds(b, 1), :].rearrange("p b d -> p (b d)"), ACT.Relu,
                                     bias=shift[:, bass.ds(b, 1)], scale=rstd[:, bass.ds(b, 1)]).then_inc(s_hn, 1)

            def h_hi(b, u):
                after(act, s_hT, b)
                after(act, s_kqp, b - NRING)
                nc.scalar.activation(hT_hi[:, u, :], p_turn[:, u, 0:D], ACT.Copy).then_inc(s_hhi, 1)

            def round_q(b, u):
                after(act, s_kq, b)
                stored(act, b, u)
                nc.scalar.activation(q_hi[:, u, :], kq[:, u, D:2 * D], ACT.Copy).then_inc(s_qhi, 1)

            make_h(0, 0)
            make_h(1, 1)
            h_hi(0, 0)
            with act.Fori(1, BLOCKS // NRING) as it:
                make_h(NRING * it, 0)
                h_hi(NRING * it - 1, 1)
                round_q(NRING * it - 2, 0)
                make_h(NRING * it + 1, 1)
                h_hi(NRING * it, 0)
                round_q(NRING * it - 1, 1)
            h_hi(BLOCKS - 1, 1)
            round_q(BLOCKS - 2, 0)
            round_q(BLOCKS - 1, 1)

            def copy_idx(it, u):
                _, slot, n, _, gb = visit(it, u)
                after(act, s_pre, n - 4)
                nc.scalar.copy(idx[:, slot, :], src_idx[:, bass.ds(gb * UNROLL + slot, 1), :]
                               .rearrange("p a t -> p (a t)")).then_inc(s_idx, 1)

            def edge_high(it, u):
                body, slot, n, _, _ = visit(it, u)
                act.wait_ge(s_edge[slot], 16 * (body + 1))
                after(act, s_prod, n - 2)
                nc.scalar.activation(edge_hi[:, slot % 2], edge[:, slot], ACT.Copy).then_inc(s_ehi, 1)

            def message_high(it, u):
                _, slot, n, _, _ = visit(it, u)
                after(act, s_pre, n)
                after(act, s_sum, n - 2)
                nc.scalar.activation(m_hi[:, slot % 2, :], pre[:, slot % 2, :], ACT.Relu).then_inc(s_mhi, 1)

            def take_sum(it, u):
                _, slot, n, _, _ = visit(it, u)
                after(act, s_sum, n)
                after(act, s_turn, n - 2)
                nc.scalar.activation(part[:, slot % 2, :], p_sum[:, slot % 2, 0:D], ACT.Copy)\
                    .then_inc(s_part, 1)

            def steps(it, first=False, last=False):
                for u in range(UNROLL):
                    if not (first and u == 0):
                        take_sum(it, u - 1)
                    if not (last and u + 3 >= UNROLL):
                        copy_idx(it, u + 3)
                    if not (last and u + 2 >= UNROLL):
                        edge_high(it, u + 2)
                    message_high(it, u)

            act.wait_ge(s_lanes, 32)
            for u in range(3):
                copy_idx(0, u)
            for u in range(2):
                edge_high(0, u)
            bodies = passes_of(act)
            steps(0, first=True)
            with act.Fori(1, bodies - 1) as it:
                steps(it)
            steps(bodies - 1, last=True)
            take_sum(bodies, -1)

            def ft_high(b, u):
                after(act, s_outp, b - NRING)
                src = ft[:, :, bass.ds(b * LANES, LANES)]
                nc.scalar.activation(hT_hi[:, u, :].rearrange("p (h n) -> p h n", h=HALVES), src, ACT.Copy)\
                    .then_inc(s_fhi, 1)

            act.wait_ge(s_ft, bodies * UNROLL)
            for u in range(NRING):
                ft_high(u, u)
            with act.Fori(1, BLOCKS // NRING) as it:
                for u in range(NRING):
                    ft_high(NRING * it + u, u)

        @block.vector
        def _(dve):
            linked = {}

            def link(ins, chain=s_prep):
                linked[chain.name] = linked.get(chain.name, 0) + 1
                ins.then_inc(chain, 1)
                dve.wait_ge(chain, linked[chain.name])

            dve.wait_ge(s_dst, 16)
            link(nc.vector.tensor_reduce(top_g[:], dst_g[:], axis=AX.X, op=ALU.max))
            link(nc.vector.tensor_scalar(dst_f[:], dst_g[:], 0.0, float(FAR), ALU.is_lt, ALU.mult))
            link(nc.vector.tensor_tensor(dst_f[:], dst_f[:], dst_g[:], ALU.add))
            link(nc.vector.tensor_reduce(low_g[:], dst_f[:], axis=AX.X, op=ALU.min))

            for c in range(XPARTS):
                dve.wait_ge(s_x[c], 16)
                with dve.Fori(c * XPART, (c + 1) * XPART) as b:
                    last = nc.vector.bn_stats(stats[:, bass.ds(b, 1), :].rearrange("p b s -> p (b s)"),
                                              x_all[:, bass.ds(b, 1), :].rearrange("p b d -> p (b d)"))
                    last.then_inc(s_stats, 1)
            dve.wait_ge(s_stats, BLOCKS)
            link(nc.vector.tensor_tensor(mean2, stats[:, :, 1], stats[:, :, 4], ALU.add), s_norm)
            link(nc.vector.tensor_tensor(diff, stats[:, :, 1], stats[:, :, 4], ALU.subtract), s_norm)
            link(nc.vector.tensor_tensor(diff, diff, diff, ALU.mult), s_norm)
            link(nc.vector.tensor_tensor(var, stats[:, :, 2], stats[:, :, 5], ALU.add), s_norm)
            link(nc.vector.scalar_tensor_tensor(var, diff, D / 4.0, var, ALU.mult, ALU.add), s_norm)
            nc.vector.tensor_scalar(var, var, 1.0 / D, EPS, ALU.mult, ALU.add).then_inc(s_var, 1)
            dve.wait_ge(s_root, 1)
            link(nc.vector.reciprocal(rstd, root), s_norm)
            link(nc.vector.tensor_tensor(diff, rstd, rstd, ALU.mult), s_norm)
            link(nc.vector.tensor_tensor(diff, diff, var, ALU.mult), s_norm)
            link(nc.vector.tensor_scalar(diff, diff, -0.5, 1.5, ALU.mult, ALU.add), s_norm)
            link(nc.vector.tensor_tensor(rstd, rstd, diff, ALU.mult), s_norm)
            link(nc.vector.tensor_tensor(shift, mean2, rstd, ALU.mult), s_norm)
            nc.vector.tensor_scalar(shift, shift, -0.5, None, ALU.mult).then_inc(s_shift, 1)

            dve.wait_ge(s_wload, 16 * 8)
            nc.vector.tensor_tensor(bias[:, D:2 * D], bias[:, D:2 * D], bias_e[:], ALU.add).then_inc(s_wsplit, 1)
            dve.wait_ge(s_wsplit, 4)
            nc.vector.tensor_tensor(w_lo[:], w_raw[:], w_hi[:].bitcast(F32), ALU.subtract).then_inc(s_wsplit, 1)
            nc.vector.tensor_tensor(we_lo[:], we_raw[:], we_hi[:].bitcast(F32), ALU.subtract).then_inc(s_wsplit, 1)
            nc.vector.tensor_tensor(wr_lo[:], wr_raw[:], wr_hi[:].bitcast(F32), ALU.subtract).then_inc(s_wsplit, 1)
            dve.wait_ge(s_wsplit, 7)

            def h_lo(b, u):
                after(dve, s_hhi, b)
                after(dve, s_kqp, b - NRING)
                nc.vector.tensor_tensor(hT_lo[:, u, :], p_turn[:, u, 0:D], hT_hi[:, u, :].bitcast(F32),
                                        ALU.subtract).then_inc(s_hlo, 1)

            def add_bias(b, u):
                after(dve, s_kqp, b)
                stored(dve, b, u)
                nc.vector.tensor_tensor(kq[:, u, :], p_sum[:, u, :], bias[:], ALU.add).then_inc(s_kq, 1)

            h_lo(0, 0)
            h_lo(1, 1)
            add_bias(0, 0)

            dve.wait_ge(s_ranges, 16)
            link(nc.vector.tensor_tensor(spans[:], ranges[:, 1, :], ranges[:, 0, :], ALU.subtract))
            link(nc.vector.tensor_reduce(span[:], spans[:], axis=AX.X, op=ALU.max))
            link(nc.vector.tensor_scalar(narrow[:], span[:], float(WIN - 1), None, ALU.is_le))
            link(nc.vector.tensor_scalar(win_f[:], ranges[:, 0, :], float(NODES - WIN), narrow[:], ALU.min, ALU.mult))
            link(nc.vector.tensor_scalar(win_g[:], low_g[:], float(NODES - WIN), narrow[0:GPART, :],
                                         ALU.min, ALU.mult))
            link(nc.vector.tensor_copy(win_tab[:], win_f[:]))
            link(nc.vector.tensor_scalar(more_passes[:], narrow[:], float(1 - PASSES), float(PASSES - 1),
                                         ALU.mult, ALU.add))
            for c in range(CHUNKS):
                link(nc.vector.tensor_scalar(rel_g[:, c, :], dst_g[:, c, :], win_g[:, c:c + 1], None, ALU.subtract))
            dve.wait_ge(s_const, 2)
            link(nc.vector.tensor_scalar(lane_wrap[:], lane_id[:], float(WIN), float(WIN), ALU.is_ge, ALU.mult))
            nc.vector.tensor_scalar(lane_node[:], lane_raw[:], lane_wrap[:], None, ALU.subtract).then_inc(s_tab, 1)
            dve.wait_ge(s_lanes, 32)
            link(nc.vector.tensor_tensor(rel_idx[:], dst_idx[:],
                                         win_f[:].unsqueeze(2).to_broadcast([LANES, GROUPS, TILES]), ALU.subtract))
            dve.wait_ge(s_tab, 1)

            with dve.Fori(1, BLOCKS // NRING) as it:
                h_lo(NRING * it, 0)
                add_bias(NRING * it - 1, 1)
                h_lo(NRING * it + 1, 1)
                add_bias(NRING * it, 0)
            add_bias(BLOCKS - 1, 1)

            def edge_low(it, u):
                body, slot, n, _, _ = visit(it, u)
                after(dve, s_ehi, n)
                after(dve, s_prod, n - 2)
                nc.vector.tensor_tensor(edge_lo[:, slot % 2], edge[:, slot], edge_hi[:, slot % 2].bitcast(F32),
                                        ALU.subtract).then_inc(s_elo, 1)

            def make_pick(it, u):
                body, slot, n, ps, _ = visit(it, u)
                dve.wait_ge(s_row[slot], 16 * (body + 1))
                after(dve, s_prod, n - 2)
                nc.vector.tensor_scalar(pick[:, slot % 2, :], rel_row[:, slot, :], lane_node[:, bass.ds(ps, 1)],
                                        None, ALU.is_equal).then_inc(s_pick, 1)

            def make_send(it, u):
                body, slot, n, ps, gb = visit(it, u)
                after(dve, s_sum, n - 2)
                rel = rel_idx[:, bass.ds(gb * UNROLL + slot, 1), :].rearrange("p a t -> p (a t)")
                nc.vector.tensor_tensor(
                    send[:, slot % 2, :, 0:WIN], rel.unsqueeze(2).to_broadcast([LANES, TILES, WIN]),
                    window_cols[:, bass.ds(ps * WIN, WIN)].unsqueeze(1).to_broadcast([LANES, TILES, WIN]),
                    ALU.is_equal).then_inc(s_send, 1)

            def add_rows(it, u):
                body, slot, n, _, _ = visit(it, u)
                after(dve, s_prod, n)
                dve.wait_ge(s_rows[slot], 16 * TILES * (body + 1))
                after(dve, s_mlo, n - 2)
                nc.vector.tensor_tensor(pre[:, slot % 2, :], p_edge[:, slot % 2, :],
                                        k_rows[:, slot].rearrange("p t d -> p (t d)"), ALU.add).then_inc(s_pre, 1)

            def message_low(it, u):
                _, slot, n, _, _ = visit(it, u)
                after(dve, s_mhi, n)
                after(dve, s_sum, n - 2)
                nc.vector.scalar_tensor_tensor(m_lo[:, slot % 2, :], pre[:, slot % 2, :], 0.0,
                                               m_hi[:, slot % 2, :].bitcast(F32), ALU.max, ALU.subtract)\
                    .then_inc(s_mlo, 1)

            def add_sum(it, u):
                _, slot, n, ps, gb = visit(it, u)
                w = dve.value_load(win_tab[0:1, bass.ds(gb * UNROLL + slot, 1)], min_val=0, max_val=NODES - WIN)
                w0 = window_start(dve, w, ps)
                after(dve, s_turn, n)
                after(dve, s_ft, n - 1)
                window = ft[:, :, bass.ds(w0, WIN)]
                turned = p_turn[:, slot % 2, 0:D].rearrange("p (h n) -> p h n", h=HALVES)[:, :, 0:WIN]
                nc.vector.tensor_tensor(window, window, turned, ALU.add).then_inc(s_ft, 1)

            def steps(it, first=False, last=False):
                for u in range(UNROLL):
                    add_rows(it, u)
                    if not (last and u + 2 >= UNROLL):
                        edge_low(it, u + 2)
                        make_pick(it, u + 2)
                    make_send(it, u)
                    message_low(it, u)
                    if not (first and u == 0):
                        add_sum(it, u - 1)

            dve.wait_ge(s_const, 5)
            after(dve, s_hn, BLOCKS - 1)
            for u in range(2):
                edge_low(0, u)
                make_pick(0, u)
            nc.vector.memset(ft[:], 0.0).then_inc(s_cleared, 1)
            dve.wait_ge(s_cleared, 1)
            bodies = passes_of(dve)
            steps(0, first=True)
            with dve.Fori(1, bodies - 1) as it:
                steps(it)
            steps(bodies - 1, last=True)
            add_sum(bodies - 1, UNROLL - 1)

            def ft_low(b, u):
                after(dve, s_fhi, b)
                after(dve, s_outp, b - NRING)
                nc.vector.tensor_tensor(hT_lo[:, u, :].rearrange("p (h n) -> p h n", h=HALVES),
                                        ft[:, :, bass.ds(b * LANES, LANES)],
                                        hT_hi[:, u, :].bitcast(F32).rearrange("p (h n) -> p h n", h=HALVES),
                                        ALU.subtract).then_inc(s_flo, 1)

            def finish(b, u):
                after(dve, s_outp, b)
                after(dve, s_xbr, b)
                if not isinstance(b, int) or b >= NRING:
                    dve.wait_ge(s_out[u], 16 // NRING * (b - u))
                nc.vector.tensor_tensor(hn[:, u, :], p_sum[:, u, 0:D], kq[:, u, 0:D], ALU.add).then_inc(s_fin, 1)

            dve.wait_ge(s_ft, bodies * UNROLL)
            for u in range(NRING):
                ft_low(u, u)
            for u in range(NRING):
                finish(u, u)
                ft_low(NRING + u, u)
            with dve.Fori(1, BLOCKS // NRING - 1) as it:
                for u in range(NRING):
                    finish(NRING * it + u, u)
                    ft_low(NRING * it + NRING + u, u)
            for u in range(NRING):
                finish(BLOCKS - NRING + u, u)

        @block.tensor
        def _(pe):
            def split_product(target, a_hi, a_lo, b_hi, b_lo, stop=True):
                for h in range(HALVES):
                    for n, (a, b) in enumerate(((a_hi, b_hi), (a_hi, b_lo), (a_lo, b_hi))):
                        ins = nc.tensor.matmul(target, a(h), b[:, h, :], start=(h == 0 and n == 0),
                                               stop=(stop and h == HALVES - 1 and n == 2))
                return ins

            def turn_h(b, u):
                after(pe, s_hn, b)
                after(pe, s_hlo, b - NRING)
                for h in range(HALVES):
                    ins = nc.tensor.transpose(p_turn[:, u, h * LANES:(h + 1) * LANES],
                                              hn[:, u, h * LANES:(h + 1) * LANES], ident[:])
                ins.then_inc(s_hT, 1)

            def node_product(b, u):
                after(pe, s_hhi, b)
                after(pe, s_hlo, b)
                after(pe, s_kq, b - NRING)
                split_product(p_sum[:, u, :], lambda h: hT_hi[:, u, h * LANES:(h + 1) * LANES],
                              lambda h: hT_lo[:, u, h * LANES:(h + 1) * LANES], w_hi, w_lo).then_inc(s_kqp, 1)

            pe.wait_ge(s_const, 3)
            turn_h(0, 0)
            pe.wait_ge(s_wsplit, 7)
            turn_h(1, 1)
            node_product(0, 0)
            with pe.Fori(1, BLOCKS // NRING) as it:
                turn_h(NRING * it, 0)
                node_product(NRING * it - 1, 1)
                turn_h(NRING * it + 1, 1)
                node_product(NRING * it, 0)
            node_product(BLOCKS - 1, 1)

            def edge_product(it, u):
                body, slot, n, _, _ = visit(it, u)
                after(pe, s_ehi, n)
                after(pe, s_elo, n)
                after(pe, s_pick, n)
                pe.wait_ge(s_win[slot], 32 * (body + 1))
                after(pe, s_pre, n - 2)
                for j in range(TILES):
                    target = p_edge[:, slot % 2, j * D:(j + 1) * D]
                    tile = slice(j * LANES, (j + 1) * LANES)
                    split_product(target, lambda h: edge_hi[:, slot % 2, h, tile],
                                  lambda h: edge_lo[:, slot % 2, h, tile], we_hi, we_lo, stop=False)
                    ins = nc.tensor.matmul(target, pick[:, slot % 2, tile], q_win[:, slot, :],
                                           start=False, stop=True)
                ins.then_inc(s_prod, 1)

            def turn_part(it, u):
                _, slot, n, _, _ = visit(it, u)
                after(pe, s_part, n)
                after(pe, s_ft, n - 2)
                for h in range(HALVES):
                    ins = nc.tensor.transpose(p_turn[:, slot % 2, h * LANES:(h + 1) * LANES],
                                              part[:, slot % 2, h * LANES:(h + 1) * LANES], ident[:])
                ins.then_inc(s_turn, 1)

            def window_sum(it, u):
                _, slot, n, _, _ = visit(it, u)
                after(pe, s_send, n)
                after(pe, s_mhi, n)
                after(pe, s_mlo, n)
                after(pe, s_part, n - 2)
                for j in range(TILES):
                    for m in (m_hi, m_lo):
                        ins = nc.tensor.matmul(p_sum[:, slot % 2, 0:D], send[:, slot % 2, j, :],
                                               m[:, slot % 2, j * D:(j + 1) * D],
                                               start=(j == 0 and m is m_hi), stop=(j == TILES - 1 and m is m_lo))
                ins.then_inc(s_sum, 1)

            def steps(it, first=False, last=False):
                for u in range(UNROLL):
                    if not (last and u + 1 >= UNROLL):
                        edge_product(it, u + 1)
                    if not (first and u == 0):
                        turn_part(it, u - 1)
                    window_sum(it, u)

            bodies = passes_of(pe)
            edge_product(0, 0)
            steps(0, first=True)
            with pe.Fori(1, bodies - 1) as it:
                steps(it)
            steps(bodies - 1, last=True)
            turn_part(bodies - 1, UNROLL - 1)

            def out_product(b, u):
                after(pe, s_fhi, b)
                after(pe, s_flo, b)
                after(pe, s_fin, b - NRING)
                split_product(p_sum[:, u, 0:D], lambda h: hT_hi[:, u, h * LANES:(h + 1) * LANES],
                              lambda h: hT_lo[:, u, h * LANES:(h + 1) * LANES], wr_hi, wr_lo).then_inc(s_outp, 1)

            for u in range(NRING):
                out_product(u, u)
            with pe.Fori(1, BLOCKS // NRING) as it:
                for u in range(NRING):
                    out_product(NRING * it + u, u)


def kernel(x, src, dst, edge_attr_256, L0_gnn_Wq, L0_gnn_bq, L0_gnn_Wk, L0_gnn_bk, L0_gnn_We, L0_gnn_be,
           L0_gnn_Wr, L0_gnn_br):
    import concourse.bacc as bacc
    from concourse.bass_utils import run_bass_kernel_spmd

    padded = GROUPS * GROUP
    x_rows = np.zeros((ROWS, D), np.float32)
    x_rows[:NODES] = x
    src_all = np.zeros((padded,), np.int32)
    src_all[:EDGES] = src
    dst_all = np.full((padded,), NO_NODE, np.int32)
    dst_all[:EDGES] = dst
    edge_all = np.zeros((padded, D), np.float32)
    edge_all[:EDGES] = edge_attr_256
    by_lane = lambda a: np.ascontiguousarray(a.reshape(GROUPS, TILES, LANES).transpose(2, 0, 1))
    arrays = {
        "x": x_rows,
        "dst_groups": dst_all.reshape(GROUPS, GROUP),
        "dst_lanes": by_lane(dst_all),
        "src_lanes": by_lane(src_all),
        "edges": np.ascontiguousarray(edge_all.reshape(GROUPS, GROUP, HALVES, LANES).transpose(0, 3, 2, 1)),
        "Wq": L0_gnn_Wq, "bq": L0_gnn_bq, "Wk": L0_gnn_Wk, "bk": L0_gnn_bk,
        "We": L0_gnn_We, "be": L0_gnn_be, "Wr": L0_gnn_Wr, "br": L0_gnn_br,
    }
    arrays = {f"in_{name}": np.ascontiguousarray(a) for name, a in arrays.items()}
    nc = bacc.Bacc("TRN2", target_bir_lowering=False, num_devices=1)
    args = [nc.dram_tensor(name, a.shape, mybir.dt.from_np(a.dtype), kind="ExternalInput").ap()
            for name, a in arrays.items()]
    out = nc.dram_tensor("out_rows", (ROWS, D), mybir.dt.float32, kind="ExternalOutput").ap()
    gnn_program(nc, *args, out)
    result = run_bass_kernel_spmd(nc, [arrays], core_ids=[0])
    return result.results[0]["out_rows"][:NODES]
```

```python
import numpy as np
import concourse.bass as bass
from concourse import mybir
from contextlib import ExitStack

LANES = 128
NODES = 6250
EDGES = 106250
D = 256
HALVES = D // LANES
BLOCKS = 52
ROWS = BLOCKS * LANES
TILES = 4
GROUP = TILES * LANES
GROUPS = -(-EDGES // GROUP)
UNROLL = 4
BODIES = GROUPS // UNROLL
CHUNKS = 2
GPART = GROUPS // CHUNKS
WIN = 48
PASSES = -(-NODES // WIN)
NO_NODE = -1
FAR = 1 << 20
EPS = 1e-5
XPARTS = 4
XPART = BLOCKS // XPARTS
NRING = 4
TURNS = BLOCKS // NRING
PAIRS = NRING // 2
OUT_SLOTS = 4
assert BLOCKS % NRING == 0 and BLOCKS % XPARTS == 0
assert GROUPS % UNROLL == 0 and GROUPS % CHUNKS == 0 and PASSES * WIN <= ROWS


def gnn_program(nc, x, dst_groups, dst_lanes, src_lanes, edges, Wq, bq, Wk, bk, We, be, Wr, br, out):
    F32, F32R = mybir.dt.float32, mybir.dt.float32r
    I32, I16 = mybir.dt.int32, mybir.dt.int16
    ALU, ACT, AX = mybir.AluOpType, mybir.ActivationFunctionType, mybir.AxisListType

    k_table = nc.dram_tensor("k_table", (ROWS, D), F32, kind="Internal").ap()
    q_table = nc.dram_tensor("q_table", (2, ROWS, D), F32R, kind="Internal").ap()
    rel_table = nc.dram_tensor("rel_table", (GROUPS, GROUP), I16, kind="Internal").ap()
    range_table = nc.dram_tensor("range_table", (2, GROUPS), F32, kind="Internal").ap()

    x_blocks = x.rearrange("(b p) d -> b p d", p=LANES)
    out_blocks = out.rearrange("(b p) d -> b p d", p=LANES)
    k_blocks = k_table.rearrange("(b p) d -> b p d", p=LANES)
    q_blocks = q_table.rearrange("s (b p) d -> s b p d", p=LANES)

    ctx = ExitStack()
    with ctx:
        def sb(name, shape, dt):
            return ctx.enter_context(nc.sbuf_tensor(name, shape, dt))

        def pb(name, shape):
            return ctx.enter_context(nc.psum_tensor(name, shape, F32))

        def sem(name):
            return ctx.enter_context(nc.semaphore(name))

        ident = sb("ident", [LANES, LANES], F32)
        window_cols = sb("window_cols", [LANES, PASSES * WIN], I16)
        lane_raw = sb("lane_raw", [2 * WIN, PASSES], F32)
        lane_wrap = sb("lane_wrap", [2 * WIN, 1], F32)
        lane_node = sb("lane_node", [2 * WIN, PASSES], F32)
        lane_id = sb("lane_id", [2 * WIN, 1], F32)
        src_idx = sb("src_idx", [LANES, GROUPS, TILES], I32)
        dst_idx = sb("dst_idx", [LANES, GROUPS, TILES], I32)
        rel_idx = sb("rel_idx", [LANES, GROUPS, TILES], F32)
        rel_g = sb("rel_g", [GPART, CHUNKS, GROUP], I16)
        top_g = sb("top_g", [GPART, CHUNKS], F32)
        low_g = sb("low_g", [GPART, CHUNKS], F32)
        win_g = sb("win_g", [GPART, CHUNKS], F32)
        ranges = sb("ranges", [LANES, 2, GROUPS], F32)
        spans = sb("spans", [LANES, GROUPS], F32)
        span = sb("span", [LANES, 1], F32)
        narrow = sb("narrow", [LANES, 1], F32)
        win_f = sb("win_f", [LANES, GROUPS], F32)
        win_tab = sb("win_tab", [LANES, GROUPS], I32)
        more_passes = sb("more_passes", [LANES, 1], I32)

        w_hi = sb("w_hi", [LANES, HALVES, 2 * D], F32R)
        w_lo = sb("w_lo", [LANES, HALVES, 2 * D], F32R)
        we_hi = sb("we_hi", [LANES, HALVES, D], F32R)
        we_lo = sb("we_lo", [LANES, HALVES, D], F32R)
        wr_hi = sb("wr_hi", [LANES, HALVES, D], F32R)
        wr_lo = sb("wr_lo", [LANES, HALVES, D], F32R)
        bias = sb("bias", [LANES, 2 * D], F32)
        bias_e = sb("bias_e", [LANES, D], F32)
        bias_r = sb("bias_r", [LANES, D], F32)

        stats = sb("stats", [LANES, BLOCKS, 6], F32)
        norm = sb("norm", [LANES, 6, BLOCKS], F32)
        mean2, diff, var, root, rstd, shift = (norm[:, i, :] for i in range(6))
        hn = sb("hn", [LANES, NRING, D], F32)
        hT_hi = sb("hT_hi", [LANES, NRING, D], F32R)
        hT_lo = sb("hT_lo", [LANES, NRING, D], F32R)

        ft = sb("ft", [LANES, HALVES, ROWS], F32)
        edge = sb("edge", [LANES, 4, HALVES, GROUP], F32)
        edge_hi = sb("edge_hi", [LANES, 2, HALVES, GROUP], F32R)
        edge_lo = sb("edge_lo", [LANES, 2, HALVES, GROUP], F32R)
        k_rows = sb("k_rows", [LANES, 4, TILES, D], F32)
        idx = sb("idx", [LANES, 4, TILES], I32)
        q_win = sb("q_win", [2 * WIN, 4, D], F32R)
        rel_row = sb("rel_row", [2 * WIN, 4, GROUP], I16)
        gap = sb("gap", [2 * WIN, GROUP], I16)
        pick = sb("pick", [2 * WIN, 2, GROUP], F32R)
        send = sb("send", [LANES, 2, TILES, LANES], F32R)
        pre = sb("pre", [LANES, 2, TILES * D], F32)
        m_hi = sb("m_hi", [LANES, 2, TILES * D], F32R)
        m_lo = sb("m_lo", [LANES, 2, TILES * D], F32R)
        x_all = ft[:].rearrange("p h r -> p (h r)").rearrange("p (b d) -> p b d", d=D)
        xo = edge[:].rearrange("p s h e -> p s (h e)").rearrange("p s (b d) -> p s b d", d=D)
        result = k_rows
        kq = k_rows[:, 0:2].rearrange("p s t d -> p (s t d)").rearrange("p (b n) -> p b n", n=2 * D)
        q_hi = m_hi[:, 0].rearrange("p (b d) -> p b d", d=D)
        q_lo = m_lo[:, 0].rearrange("p (b d) -> p b d", d=D)
        dst_g = pre[0:GPART, 0, :].bitcast(I32).rearrange("p (c e) -> p c e", c=CHUNKS)
        dst_f = pre[0:GPART, 1, :].rearrange("p (c e) -> p c e", c=CHUNKS)
        w_raw = k_rows[:, 2].rearrange("p t d -> p (t d)").rearrange("p (h n) -> p h n", h=HALVES)
        we_raw = k_rows[:, 3, 0:HALVES]
        wr_raw = k_rows[:, 3, HALVES:2 * HALVES]
        part = sb("part", [LANES, 2, D], F32)

        p_edge = pb("p_edge", [LANES, 2, TILES * D])
        p_sum = pb("p_sum", [LANES, 2, 512])
        p_turn = pb("p_turn", [LANES, 2, 512])

        s_dst = sem("dst_loaded")
        s_lanes = sem("lanes_loaded")
        s_wload = sem("weights_loaded")
        s_range = sem("range_stored")
        s_ranges = sem("ranges_loaded")
        s_rel = sem("rel_stored")
        s_prep = sem("prep_step")
        s_tab = sem("window_table_ready")
        s_wsplit = sem("weights_split")
        s_zero = sem("zeroed")
        s_const = sem("constants_ready")
        s_x = [sem(f"x_loaded_{c}") for c in range(XPARTS)]
        s_norm = sem("layernorm_step")
        s_var = sem("variance_ready")
        s_root = sem("deviation_ready")
        s_shift = sem("scale_and_shift_ready")
        s_stats = sem("row_statistics_ready")
        s_cleared = sem("ft_cleared")
        s_hn = sem("hn_ready")
        s_hT = sem("h_transposed")
        s_hhi = sem("hT_hi_ready")
        s_hlo = sem("hT_lo_ready")
        s_kqp = sem("kq_product_done")
        s_kq = sem("kq_ready")
        s_qhi = sem("q_hi_ready")
        s_qlo = sem("q_lo_ready")
        s_store = [sem(f"tables_stored_{u}") for u in range(NRING)]
        s_edge = [sem(f"edge_loaded_{u}") for u in range(UNROLL)]
        s_row = [sem(f"rel_row_loaded_{u}") for u in range(UNROLL)]
        s_win = [sem(f"q_window_loaded_{u}") for u in range(UNROLL)]
        s_rows = [sem(f"k_rows_gathered_{u}") for u in range(UNROLL)]
        s_go = sem("gathers_may_start")
        s_go_act = sem("scalar_may_go_on")
        s_idx = sem("idx_ready")
        s_ehi = sem("edge_hi_ready")
        s_elo = sem("edge_lo_ready")
        s_gap = sem("gap_ready")
        s_pick = sem("pick_ready")
        s_send = sem("send_ready")
        s_prod = sem("edge_product_done")
        s_pre = sem("pre_ready")
        s_mhi = sem("m_hi_ready")
        s_mlo = sem("m_lo_ready")
        s_sum = sem("sum_done")
        s_part = sem("part_ready")
        s_turn = sem("part_transposed")
        s_ft = sem("ft_added")
        s_xo = [sem(f"xo_loaded_{u}") for u in range(OUT_SLOTS)]
        s_fhi = sem("ft_hi_ready")
        s_flo = sem("ft_lo_ready")
        s_outp = sem("out_product_done")
        s_xbr = sem("x_plus_br_ready")
        s_fin = sem("out_ready")
        s_out = [sem(f"out_stored_{u}") for u in range(2)]
        s_free = sem("out_slot_free")

        def after(eng, semaphore, n):
            if isinstance(n, int) and n < 0:
                return
            eng.wait_ge(semaphore, n + 1)

        def stored(eng, b, u):
            if isinstance(b, int) and b < NRING:
                return
            eng.wait_ge(s_store[u], 3 * 16 // NRING * (b - u))

        def one(t, b):
            return t[:, bass.ds(b, 1), :].rearrange("p b d -> p (b d)")

        def visit(it, u):
            body, slot = it + u // UNROLL, u % UNROLL
            return body, slot, body * UNROLL + slot, body // BODIES, body % BODIES

        def window_start(eng, w, ps):
            return nc.s_assert_within(eng.snap(w + ps * WIN), 0, ROWS - WIN, skip_runtime_bounds_check_because=(
                "either there is one pass, or the window table is all zeros"))

        def passes_of(eng):
            eng.wait_ge(s_tab, 1)
            return eng.value_load(more_passes[0:1, 0:1], min_val=0, max_val=PASSES - 1) * BODIES + BODIES

        PREP_STEPS = 4 + 3 + 4 + CHUNKS + 2

        block = ctx.enter_context(nc.Block())

        @block.sync
        def _(sp):
            sp.dma_start(dst_g[:], dst_groups.rearrange("(p c) e -> p c e", c=CHUNKS)).then_inc(s_dst, 16)

            for c in range(XPARTS):
                blocks = slice(c * XPART, (c + 1) * XPART)
                sp.dma_start(x_all[:, blocks, :], x_blocks[blocks].rearrange("b p d -> p b d")).then_inc(s_x[c], 16)
            for w_ap, dst in ((Wk, w_raw[:, :, 0:D]), (Wq, w_raw[:, :, D:2 * D])):
                sp.dma_start(dst, w_ap.rearrange("(h p) n -> p h n", p=LANES)).then_inc(s_wload, 16)
            sp.dma_start(we_raw[:], We.rearrange("(h p) n -> p h n", p=LANES)).then_inc(s_wload, 16)
            sp.dma_start(wr_raw[:], Wr.rearrange("(h p) n -> p h n", p=LANES)).then_inc(s_wload, 16)
            for b_ap, dst in ((bk, bias[:, 0:D]), (bq, bias[:, D:2 * D]), (be, bias_e[:]), (br, bias_r[:])):
                sp.dma_start(dst, b_ap.rearrange("(a n) -> a n", a=1).to_broadcast([LANES, D]))\
                    .then_inc(s_wload, 16)
            sp.dma_start(dst_idx[:], dst_lanes).then_inc(s_lanes, 16)
            sp.dma_start(src_idx[:], src_lanes).then_inc(s_lanes, 16)
            sp.wait_ge(s_prep, 4)
            sp.dma_start(range_table[0].rearrange("(p c) -> p c", c=CHUNKS), low_g[:]).then_inc(s_range, 16)
            sp.dma_start(range_table[1].rearrange("(p c) -> p c", c=CHUNKS), top_g[:]).then_inc(s_range, 16)
            sp.wait_ge(s_range, 32)
            sp.dma_start(ranges[:], range_table.unsqueeze(0).to_broadcast([LANES, 2, GROUPS]))\
                .then_inc(s_ranges, 16)

            def store_tables(b, u):
                after(sp, s_kq, b)
                after(sp, s_qhi, b)
                after(sp, s_qlo, b)

                def at(t):
                    return t[b] if isinstance(b, int) else t[bass.ds(b, 1)].rearrange("a p d -> (a p) d")
                sp.dma_start(at(k_blocks), kq[:, u, 0:D]).then_inc(s_store[u], 16)
                sp.dma_start(at(q_blocks[0]).bitcast(F32), q_hi[:, u, :].bitcast(F32)).then_inc(s_store[u], 16)
                sp.dma_start(at(q_blocks[1]).bitcast(F32), q_lo[:, u, :].bitcast(F32)).then_inc(s_store[u], 16)

            def load_edge(it, u):
                body, slot, n, _, gb = visit(it, u)
                after(sp, s_ehi, n - 4)
                after(sp, s_elo, n - 4)
                g = gb * UNROLL + slot
                src = edges[g] if isinstance(g, int) else edges[bass.ds(g, 1)].rearrange("a p h e -> (a p) h e")
                sp.dma_start(edge[:, slot], src).then_inc(s_edge[slot], 16)

            for u in range(UNROLL):
                load_edge(0, u)
            sp.wait_ge(s_prep, PREP_STEPS - 2)
            sp.dma_start(rel_table.rearrange("(p c) e -> p c e", c=CHUNKS), rel_g[:]).then_inc(s_rel, 16)
            with sp.Fori(0, TURNS) as it:
                for u in range(NRING):
                    store_tables(NRING * it + u, u)

            def load_row(it, u):
                body, slot, n, _, gb = visit(it, u)
                after(sp, s_pick, n - 4)
                g = gb * UNROLL + slot
                sp.dma_start(rel_row[:, slot, :], rel_table[bass.ds(g, 1), :].to_broadcast([2 * WIN, GROUP]))\
                    .then_inc(s_row[slot], 16)

            def load_window(it, u):
                body, slot, n, ps, gb = visit(it, u)
                g = gb * UNROLL + slot
                w = sp.value_load(win_tab[0:1, bass.ds(g, 1)], min_val=0, max_val=NODES - WIN)
                w0 = window_start(sp, w, ps)
                after(sp, s_prod, n - 4)
                for s in range(2):
                    sp.dma_start(q_win[s * WIN:(s + 1) * WIN, slot, :].bitcast(F32),
                                 q_table[s, bass.ds(w0, WIN), :].bitcast(F32)).then_inc(s_win[slot], 16)

            sp.wait_ge(s_rel, 16)
            for u in range(UNROLL):
                load_row(0, u)
            bodies = passes_of(sp)
            for u in range(NRING):
                sp.wait_ge(s_store[u], 16 * 3 * TURNS)
            for u in range(UNROLL):
                load_window(0, u)
            with sp.Fori(1, bodies) as it:
                for u in range(UNROLL):
                    load_edge(it, u)
                    load_row(it, u)
                    load_window(it, u)

            def load_xo(t):
                sp.dma_start(xo[:, t % OUT_SLOTS], x_blocks[NRING * t:NRING * (t + 1)].rearrange("b p d -> p b d"))\
                    .then_inc(s_xo[t % OUT_SLOTS], 16)

            for t in range(OUT_SLOTS):
                sp.wait_ge(s_ehi, bodies * UNROLL - (UNROLL - 1) + t)
                sp.wait_ge(s_elo, bodies * UNROLL - (UNROLL - 1) + t)
                load_xo(t)
            for t in range(TURNS):
                after(sp, s_fin, PAIRS * (t + 1) - 1)
                sp.dma_start(out_blocks[NRING * t:NRING * (t + 1)].rearrange("b p d -> p b d"),
                             result[:, t % OUT_SLOTS]).then_inc(s_out[t % 2], 16)
                if t + OUT_SLOTS < TURNS:
                    load_xo(t + OUT_SLOTS)
                if t > 0:
                    sp.wait_ge(s_out[(t - 1) % 2], 16 * ((t - 1) // 2 + 1))
                    sp.sem_inc(s_free, 1)
            sp.wait_ge(s_out[(TURNS - 1) % 2], 16 * ((TURNS - 1) // 2 + 1))

        @block.gpsimd
        def _(pool):
            nc.gpsimd.memset(ident[:], 0.0).then_inc(s_zero, 1)
            nc.gpsimd.iota(lane_raw[:], pattern=[[WIN, PASSES]], base=0, channel_multiplier=1,
                           allow_small_or_imprecise_dtypes=True).then_inc(s_const, 1)
            nc.gpsimd.iota(lane_id[:], pattern=[[0, 1]], base=0, channel_multiplier=1,
                           allow_small_or_imprecise_dtypes=True).then_inc(s_const, 1)
            pool.wait_ge(s_zero, 1)
            nc.gpsimd.affine_select(out=ident[:], in_=ident[:], compare_op=ALU.not_equal, fill=1.0, base=0,
                                    pattern=[[-1, LANES]], channel_multiplier=1).then_inc(s_const, 1)
            nc.gpsimd.iota(window_cols[:], pattern=[[1, PASSES * WIN]], base=0, channel_multiplier=0,
                           allow_small_or_imprecise_dtypes=True).then_inc(s_const, 1)
            nc.gpsimd.memset(send[:].bitcast(F32), 0.0).then_inc(s_const, 1)

            def make_q_lo(b, u):
                after(pool, s_qhi, b)
                stored(pool, b, u)
                nc.gpsimd.tensor_tensor(q_lo[:, u, :], kq[:, u, D:2 * D], q_hi[:, u, :].bitcast(F32),
                                        ALU.subtract).then_inc(s_qlo, 1)

            for b in range(NRING):
                make_q_lo(b, b)
            with pool.Fori(1, TURNS) as it:
                for u in range(NRING):
                    make_q_lo(NRING * it + u, u)

            bodies = passes_of(pool)
            for u in range(NRING):
                pool.wait_ge(s_store[u], 48 * TURNS)

            def gather(it, u):
                _, slot, n, _, _ = visit(it, u)
                after(pool, s_idx, n)
                after(pool, s_pre, n - 4)
                pool.sem_inc(s_go, 1)
                for j in range(TILES):
                    nc.gpsimd.indirect_dma_start(
                        out=k_rows[:, slot, j, :], out_offset=None, in_=k_table,
                        in_offset=bass.IndirectOffsetOnAxis(ap=idx[:, slot, j:j + 1], axis=0),
                    ).then_inc(s_rows[slot], 16)

            for u in range(UNROLL):
                gather(0, u)
            with pool.Fori(1, bodies) as it:
                for u in range(UNROLL):
                    gather(it, u)

            for t in range(TURNS):
                pool.wait_ge(s_xo[t % OUT_SLOTS], 16 * (t // OUT_SLOTS + 1))
                turn_x = xo[:, t % OUT_SLOTS]
                nc.gpsimd.tensor_tensor(turn_x, turn_x, bias_r[:].unsqueeze(1).to_broadcast([LANES, NRING, D]),
                                        ALU.add).then_inc(s_xbr, 1)

        @block.scalar
        def _(act):
            act.wait_ge(s_wload, 16 * 8)
            nc.scalar.activation(w_hi[:], w_raw[:], ACT.Copy).then_inc(s_wsplit, 1)
            nc.scalar.activation(we_hi[:], we_raw[:], ACT.Copy).then_inc(s_wsplit, 1)
            nc.scalar.activation(wr_hi[:], wr_raw[:], ACT.Copy).then_inc(s_wsplit, 1)

            act.wait_ge(s_var, 1)
            nc.scalar.activation(root, var, ACT.Sqrt).then_inc(s_root, 1)
            act.wait_ge(s_shift, 1)

            def make_h(b, u):
                after(act, s_hT, b - NRING)
                act.sem_inc(s_go_act, 1)
                nc.scalar.activation(hn[:, u, :], one(x_all, b), ACT.Relu,
                                     bias=shift[:, bass.ds(b, 1)], scale=rstd[:, bass.ds(b, 1)]).then_inc(s_hn, 1)

            def h_hi(b, u):
                after(act, s_hT, b)
                after(act, s_kqp, b - NRING)
                nc.scalar.activation(hT_hi[:, u, :], p_turn[:, u % 2, 0:D], ACT.Copy).then_inc(s_hhi, 1)

            def round_q(b, u):
                after(act, s_kq, b)
                stored(act, b, u)
                nc.scalar.activation(q_hi[:, u, :], kq[:, u, D:2 * D], ACT.Copy).then_inc(s_qhi, 1)

            def node_step(t, u, first=False, last=False):
                b = NRING * t + u
                if not (last and u + 3 >= NRING):
                    make_h(b + 3, (u + 3) % NRING)
                if not (last and u + 1 >= NRING):
                    h_hi(b + 1, (u + 1) % NRING)
                if not (first and u < 1):
                    round_q(b - 1, (u - 1) % NRING)

            for u in range(3):
                make_h(u, u)
            h_hi(0, 0)
            for u in range(NRING):
                node_step(0, u, first=True)
            with act.Fori(1, TURNS - 1) as it:
                for u in range(NRING):
                    node_step(it, u)
            for u in range(NRING):
                node_step(TURNS - 1, u, last=True)
            round_q(BLOCKS - 1, NRING - 1)

            def copy_idx(it, u):
                _, slot, n, _, gb = visit(it, u)
                after(act, s_pre, n - 4)
                nc.scalar.copy(idx[:, slot, :], src_idx[:, bass.ds(gb * UNROLL + slot, 1), :]
                               .rearrange("p a t -> p (a t)")).then_inc(s_idx, 1)

            def edge_high(it, u):
                body, slot, n, _, _ = visit(it, u)
                act.wait_ge(s_edge[slot], 16 * (body + 1))
                after(act, s_prod, n - 2)
                nc.scalar.activation(edge_hi[:, slot % 2], edge[:, slot], ACT.Copy).then_inc(s_ehi, 1)

            def make_pick(it, u):
                body, slot, n, ps, _ = visit(it, u)
                act.wait_ge(s_row[slot], 16 * (body + 1))
                after(act, s_prod, n - 2)
                after(act, s_pick, n - 1)
                act.sem_inc(s_go_act, 1)
                nc.scalar.activation(gap[:], rel_row[:, slot, :], ACT.Abs, scale=-1.0,
                                     bias=lane_node[:, bass.ds(ps, 1)]).then_inc(s_gap, 1)
                after(act, s_gap, n)
                nc.scalar.activation(pick[:, slot % 2, :], gap[:], ACT.Relu, bias=1.0, scale=-1.0)\
                    .then_inc(s_pick, 1)

            def message_high(it, u):
                _, slot, n, _, _ = visit(it, u)
                after(act, s_pre, n)
                after(act, s_sum, n - 2)
                nc.scalar.activation(m_hi[:, slot % 2, :], pre[:, slot % 2, :], ACT.Relu).then_inc(s_mhi, 1)

            def take_sum(it, u):
                _, slot, n, _, _ = visit(it, u)
                after(act, s_sum, n)
                after(act, s_turn, n - 2)
                nc.scalar.activation(part[:, slot % 2, :], p_sum[:, slot % 2, 0:D], ACT.Copy)\
                    .then_inc(s_part, 1)

            def steps(it, first=False, last=False):
                for u in range(UNROLL):
                    if not (last and u + 3 >= UNROLL):
                        copy_idx(it, u + 3)
                    if not (last and u + 2 >= UNROLL):
                        edge_high(it, u + 2)
                    message_high(it, u)
                    if not (last and u + 2 >= UNROLL):
                        make_pick(it, u + 2)
                    if not (first and u < 2):
                        take_sum(it, u - 2)

            act.wait_ge(s_lanes, 32)
            for u in range(3):
                copy_idx(0, u)
            for u in range(2):
                edge_high(0, u)
            bodies = passes_of(act)
            for u in range(2):
                make_pick(0, u)
            steps(0, first=True)
            with act.Fori(1, bodies - 1) as it:
                steps(it)
            steps(bodies - 1, last=True)
            take_sum(bodies - 1, UNROLL - 2)
            take_sum(bodies - 1, UNROLL - 1)

            def ft_high(b, u):
                after(act, s_outp, b - NRING)
                act.sem_inc(s_go_act, 1)
                nc.scalar.activation(hT_hi[:, u, :].rearrange("p (h n) -> p h n", h=HALVES),
                                     ft[:, :, bass.ds(b * LANES, LANES)], ACT.Copy).then_inc(s_fhi, 1)

            act.wait_ge(s_ft, bodies * UNROLL)
            for u in range(NRING):
                ft_high(u, u)
            with act.Fori(1, TURNS) as it:
                for u in range(NRING):
                    ft_high(NRING * it + u, u)

        @block.vector
        def _(dve):
            linked = {}

            def link(ins, chain=s_prep):
                linked[chain.name] = linked.get(chain.name, 0) + 1
                ins.then_inc(chain, 1)
                dve.wait_ge(chain, linked[chain.name])

            dve.wait_ge(s_dst, 16)
            link(nc.vector.tensor_reduce(top_g[:], dst_g[:], axis=AX.X, op=ALU.max))
            link(nc.vector.tensor_scalar(dst_f[:], dst_g[:], 0.0, float(FAR), ALU.is_lt, ALU.mult))
            link(nc.vector.tensor_tensor(dst_f[:], dst_f[:], dst_g[:], ALU.add))
            link(nc.vector.tensor_reduce(low_g[:], dst_f[:], axis=AX.X, op=ALU.min))

            for c in range(XPARTS):
                dve.wait_ge(s_x[c], 16)
                for b in range(c * XPART, (c + 1) * XPART):
                    nc.vector.bn_stats(stats[:, b, :], x_all[:, b, :]).then_inc(s_stats, 1)
            dve.wait_ge(s_stats, BLOCKS)
            link(nc.vector.tensor_tensor(mean2, stats[:, :, 1], stats[:, :, 4], ALU.add), s_norm)
            link(nc.vector.tensor_tensor(diff, stats[:, :, 1], stats[:, :, 4], ALU.subtract), s_norm)
            link(nc.vector.tensor_tensor(diff, diff, diff, ALU.mult), s_norm)
            link(nc.vector.tensor_tensor(var, stats[:, :, 2], stats[:, :, 5], ALU.add), s_norm)
            link(nc.vector.scalar_tensor_tensor(var, diff, D / 4.0, var, ALU.mult, ALU.add), s_norm)
            nc.vector.tensor_scalar(var, var, 1.0 / D, EPS, ALU.mult, ALU.add).then_inc(s_var, 1)
            dve.wait_ge(s_root, 1)
            link(nc.vector.reciprocal(rstd, root), s_norm)
            link(nc.vector.tensor_tensor(diff, rstd, rstd, ALU.mult), s_norm)
            link(nc.vector.tensor_tensor(diff, diff, var, ALU.mult), s_norm)
            link(nc.vector.tensor_scalar(diff, diff, -0.5, 1.5, ALU.mult, ALU.add), s_norm)
            link(nc.vector.tensor_tensor(rstd, rstd, diff, ALU.mult), s_norm)
            link(nc.vector.tensor_tensor(shift, mean2, rstd, ALU.mult), s_norm)
            nc.vector.tensor_scalar(shift, shift, -0.5, None, ALU.mult).then_inc(s_shift, 1)

            dve.wait_ge(s_wload, 16 * 8)
            nc.vector.tensor_tensor(bias[:, D:2 * D], bias[:, D:2 * D], bias_e[:], ALU.add).then_inc(s_wsplit, 1)
            dve.wait_ge(s_wsplit, 4)
            nc.vector.tensor_tensor(w_lo[:], w_raw[:], w_hi[:].bitcast(F32), ALU.subtract).then_inc(s_wsplit, 1)
            nc.vector.tensor_tensor(we_lo[:], we_raw[:], we_hi[:].bitcast(F32), ALU.subtract).then_inc(s_wsplit, 1)
            nc.vector.tensor_tensor(wr_lo[:], wr_raw[:], wr_hi[:].bitcast(F32), ALU.subtract).then_inc(s_wsplit, 1)
            dve.wait_ge(s_wsplit, 7)

            def h_lo(b, u):
                after(dve, s_hhi, b)
                after(dve, s_kqp, b - NRING)
                nc.vector.tensor_tensor(hT_lo[:, u, :], p_turn[:, u % 2, 0:D], hT_hi[:, u, :].bitcast(F32),
                                        ALU.subtract).then_inc(s_hlo, 1)

            def add_bias(b, u):
                after(dve, s_kqp, b)
                stored(dve, b, u)
                nc.vector.tensor_tensor(kq[:, u, :], p_sum[:, u % 2, :], bias[:], ALU.add).then_inc(s_kq, 1)

            def node_step(t, u, last=False):
                if not (last and u + 1 >= NRING):
                    h_lo(NRING * t + u + 1, (u + 1) % NRING)
                add_bias(NRING * t + u, u)
                if u == NRING - 1:
                    nc.vector.tensor_copy(x_all[:, bass.ds(NRING * t, NRING), :], zeros)\
                        .then_inc(s_cleared, 1)

            zeros = send[:, 0, 0:2, :].bitcast(F32).rearrange("p t n -> p (t n)").unsqueeze(1)\
                .to_broadcast([LANES, NRING, D])
            dve.wait_ge(s_const, 5)
            h_lo(0, 0)
            node_step(0, 0)

            dve.wait_ge(s_ranges, 16)
            link(nc.vector.tensor_tensor(spans[:], ranges[:, 1, :], ranges[:, 0, :], ALU.subtract))
            link(nc.vector.tensor_reduce(span[:], spans[:], axis=AX.X, op=ALU.max))
            link(nc.vector.tensor_scalar(narrow[:], span[:], float(WIN - 1), None, ALU.is_le))
            node_step(0, 1)
            nc.vector.tensor_scalar(win_f[:], ranges[:, 0, :], float(NODES - WIN), narrow[:],
                                    ALU.min, ALU.mult).then_inc(s_prep, 1)
            nc.vector.tensor_scalar(win_g[:], low_g[:], float(NODES - WIN), narrow[0:GPART, :],
                                    ALU.min, ALU.mult).then_inc(s_prep, 1)
            nc.vector.tensor_scalar(more_passes[:], narrow[:], float(1 - PASSES), float(PASSES - 1),
                                    ALU.mult, ALU.add).then_inc(s_prep, 1)
            dve.wait_ge(s_const, 2)
            nc.vector.tensor_scalar(lane_wrap[:], lane_id[:], float(WIN), float(WIN), ALU.is_ge, ALU.mult)\
                .then_inc(s_prep, 1)
            node_step(0, 2)
            dve.wait_ge(s_prep, 4 + 3 + 4)
            for c in range(CHUNKS):
                nc.vector.tensor_scalar(rel_g[:, c, :], dst_g[:, c, :], win_g[:, c:c + 1], None,
                                        ALU.subtract).then_inc(s_prep, 1)
            node_step(0, 3)
            nc.vector.tensor_copy(win_tab[:], win_f[:]).then_inc(s_prep, 1)
            nc.vector.tensor_scalar(lane_node[:], lane_raw[:], lane_wrap[:], None, ALU.subtract).then_inc(s_prep, 1)
            dve.wait_ge(s_prep, PREP_STEPS)
            dve.sem_inc(s_tab, 1)

            with dve.Fori(1, TURNS - 1) as it:
                for u in range(NRING):
                    node_step(it, u)
            for u in range(NRING):
                node_step(TURNS - 1, u, last=True)

            def edge_low(it, u):
                body, slot, n, _, _ = visit(it, u)
                after(dve, s_ehi, n)
                after(dve, s_prod, n - 2)
                nc.vector.tensor_tensor(edge_lo[:, slot % 2], edge[:, slot], edge_hi[:, slot % 2].bitcast(F32),
                                        ALU.subtract).then_inc(s_elo, 1)

            def make_send(it, u):
                body, slot, n, ps, gb = visit(it, u)
                after(dve, s_sum, n - 2)
                rel = rel_idx[:, bass.ds(gb * UNROLL + slot, 1), :].rearrange("p a t -> p (a t)")
                nc.vector.tensor_tensor(
                    send[:, slot % 2, :, 0:WIN], rel.unsqueeze(2).to_broadcast([LANES, TILES, WIN]),
                    window_cols[:, bass.ds(ps * WIN, WIN)].unsqueeze(1).to_broadcast([LANES, TILES, WIN]),
                    ALU.is_equal).then_inc(s_send, 1)

            def add_rows(it, u):
                body, slot, n, _, _ = visit(it, u)
                after(dve, s_prod, n)
                dve.wait_ge(s_rows[slot], 16 * TILES * (body + 1))
                after(dve, s_mlo, n - 2)
                nc.vector.tensor_tensor(pre[:, slot % 2, :], p_edge[:, slot % 2, :],
                                        k_rows[:, slot].rearrange("p t d -> p (t d)"), ALU.add).then_inc(s_pre, 1)

            def message_low(it, u):
                _, slot, n, _, _ = visit(it, u)
                after(dve, s_mhi, n)
                after(dve, s_sum, n - 2)
                nc.vector.scalar_tensor_tensor(m_lo[:, slot % 2, :], pre[:, slot % 2, :], 0.0,
                                               m_hi[:, slot % 2, :].bitcast(F32), ALU.max, ALU.subtract)\
                    .then_inc(s_mlo, 1)

            def add_sum(it, u):
                _, slot, n, ps, gb = visit(it, u)
                w = dve.value_load(win_tab[0:1, bass.ds(gb * UNROLL + slot, 1)], min_val=0, max_val=NODES - WIN)
                w0 = window_start(dve, w, ps)
                after(dve, s_turn, n)
                after(dve, s_ft, n - 1)
                window = ft[:, :, bass.ds(w0, WIN)]
                turned = p_turn[:, slot % 2, 0:D].rearrange("p (h n) -> p h n", h=HALVES)[:, :, 0:WIN]
                nc.vector.tensor_tensor(window, window, turned, ALU.add).then_inc(s_ft, 1)

            def steps(it, first=False, last=False):
                for u in range(UNROLL):
                    add_rows(it, u)
                    if not (last and u + 2 >= UNROLL):
                        edge_low(it, u + 2)
                    make_send(it, u)
                    message_low(it, u)
                    if not (first and u < 3):
                        add_sum(it, u - 3)

            dve.wait_ge(s_lanes, 32)
            nc.vector.tensor_tensor(rel_idx[:], dst_idx[:], win_f[:].unsqueeze(2).to_broadcast(
                [LANES, GROUPS, TILES]), ALU.subtract).then_inc(s_prep, 1)
            dve.wait_ge(s_prep, PREP_STEPS + 1)
            for u in range(2):
                edge_low(0, u)
            dve.wait_ge(s_cleared, TURNS)
            bodies = passes_of(dve)
            steps(0, first=True)
            with dve.Fori(1, bodies - 1) as it:
                steps(it)
            steps(bodies - 1, last=True)
            for u in range(UNROLL - 3, UNROLL):
                add_sum(bodies - 1, u)

            def ft_low(b, u):
                after(dve, s_fhi, b)
                after(dve, s_outp, b - NRING)
                nc.vector.tensor_tensor(hT_lo[:, u, :].rearrange("p (h n) -> p h n", h=HALVES),
                                        ft[:, :, bass.ds(b * LANES, LANES)],
                                        hT_hi[:, u, :].bitcast(F32).rearrange("p (h n) -> p h n", h=HALVES),
                                        ALU.subtract).then_inc(s_flo, 1)

            def finish(t, v):
                after(dve, s_outp, NRING * t + 2 * v + 1)
                after(dve, s_xbr, t)
                after(dve, s_free, t - OUT_SLOTS)
                slot = t % OUT_SLOTS

                def pair(a):
                    return a[:, bass.ds(slot, 1), 2 * v:2 * v + 2, :].rearrange("p s b d -> p (s b) d")
                nc.vector.tensor_tensor(pair(result), p_edge[:, v, 0:2 * D].rearrange("p (b d) -> p b d", d=D),
                                        pair(xo), ALU.add).then_inc(s_fin, 1)

            def out_step(t, u, last=False):
                if not (last and u + 2 >= NRING):
                    ft_low(NRING * t + u + 2, (u + 2) % NRING)
                if u % 2:
                    finish(t, u // 2)

            ft_low(0, 0)
            ft_low(1, 1)
            for t in range(OUT_SLOTS):
                for u in range(NRING):
                    out_step(t, u)
            with dve.Fori(OUT_SLOTS, TURNS - 1) as it:
                for u in range(NRING):
                    out_step(it, u)
            for u in range(NRING):
                out_step(TURNS - 1, u, last=True)

        @block.tensor
        def _(pe):
            def split_product(target, a_hi, a_lo, b_hi, b_lo, stop=True):
                for h in range(HALVES):
                    for n, (a, b) in enumerate(((a_hi, b_hi), (a_hi, b_lo), (a_lo, b_hi))):
                        ins = nc.tensor.matmul(target, a(h), b[:, h, :], start=(h == 0 and n == 0),
                                               stop=(stop and h == HALVES - 1 and n == 2))
                return ins

            def turn_h(b, u):
                after(pe, s_hn, b)
                after(pe, s_hlo, b - 2)
                for h in range(HALVES):
                    ins = nc.tensor.transpose(p_turn[:, u % 2, h * LANES:(h + 1) * LANES],
                                              hn[:, u, h * LANES:(h + 1) * LANES], ident[:])
                ins.then_inc(s_hT, 1)

            def node_product(b, u):
                after(pe, s_hhi, b)
                after(pe, s_hlo, b)
                after(pe, s_kq, b - 2)
                split_product(p_sum[:, u % 2, :], lambda h: hT_hi[:, u, h * LANES:(h + 1) * LANES],
                              lambda h: hT_lo[:, u, h * LANES:(h + 1) * LANES], w_hi, w_lo).then_inc(s_kqp, 1)

            pe.wait_ge(s_const, 3)
            def node_step(t, u, last=False):
                if not (last and u + 2 >= NRING):
                    turn_h(NRING * t + u + 2, (u + 2) % NRING)
                node_product(NRING * t + u, u)

            turn_h(0, 0)
            turn_h(1, 1)
            pe.wait_ge(s_wsplit, 7)
            for u in range(NRING):
                node_step(0, u)
            with pe.Fori(1, TURNS - 1) as it:
                for u in range(NRING):
                    node_step(it, u)
            for u in range(NRING):
                node_step(TURNS - 1, u, last=True)

            def edge_product(it, u):
                body, slot, n, _, _ = visit(it, u)
                after(pe, s_ehi, n)
                after(pe, s_elo, n)
                after(pe, s_pick, n)
                pe.wait_ge(s_win[slot], 32 * (body + 1))
                after(pe, s_pre, n - 2)
                for j in range(TILES):
                    target = p_edge[:, slot % 2, j * D:(j + 1) * D]
                    tile = slice(j * LANES, (j + 1) * LANES)
                    split_product(target, lambda h: edge_hi[:, slot % 2, h, tile],
                                  lambda h: edge_lo[:, slot % 2, h, tile], we_hi, we_lo, stop=False)
                    ins = nc.tensor.matmul(target, pick[:, slot % 2, tile], q_win[:, slot, :],
                                           start=False, stop=True)
                ins.then_inc(s_prod, 1)

            def turn_part(it, u):
                _, slot, n, _, _ = visit(it, u)
                after(pe, s_part, n)
                after(pe, s_ft, n - 2)
                for h in range(HALVES):
                    ins = nc.tensor.transpose(p_turn[:, slot % 2, h * LANES:(h + 1) * LANES],
                                              part[:, slot % 2, h * LANES:(h + 1) * LANES], ident[:])
                ins.then_inc(s_turn, 1)

            def window_sum(it, u):
                _, slot, n, _, _ = visit(it, u)
                after(pe, s_send, n)
                after(pe, s_mhi, n)
                after(pe, s_mlo, n)
                after(pe, s_part, n - 2)
                for j in range(TILES):
                    for m in (m_hi, m_lo):
                        ins = nc.tensor.matmul(p_sum[:, slot % 2, 0:D], send[:, slot % 2, j, :],
                                               m[:, slot % 2, j * D:(j + 1) * D],
                                               start=(j == 0 and m is m_hi), stop=(j == TILES - 1 and m is m_lo))
                ins.then_inc(s_sum, 1)

            def steps(it, first=False, last=False):
                for u in range(UNROLL):
                    if not (last and u + 1 >= UNROLL):
                        edge_product(it, u + 1)
                    if not (first and u < 1):
                        window_sum(it, u - 1)
                    if not (first and u < 2):
                        turn_part(it, u - 2)

            bodies = passes_of(pe)
            edge_product(0, 0)
            steps(0, first=True)
            with pe.Fori(1, bodies - 1) as it:
                steps(it)
            steps(bodies - 1, last=True)
            turn_part(bodies - 1, UNROLL - 2)
            window_sum(bodies - 1, UNROLL - 1)
            turn_part(bodies - 1, UNROLL - 1)

            def out_product(b, u, pair):
                after(pe, s_fhi, b)
                after(pe, s_flo, b)
                if u % 2 == 0:
                    after(pe, s_fin, pair - 2)
                split_product(p_edge[:, u // 2, (u % 2) * D:(u % 2 + 1) * D], lambda h: hT_hi[:, u, h * LANES:(h + 1) * LANES],
                              lambda h: hT_lo[:, u, h * LANES:(h + 1) * LANES], wr_hi, wr_lo).then_inc(s_outp, 1)

            for u in range(NRING):
                out_product(u, u, u // 2)
            with pe.Fori(1, TURNS) as it:
                for u in range(NRING):
                    out_product(NRING * it + u, u, PAIRS * it + u // 2)


def kernel(x, src, dst, edge_attr_256, L0_gnn_Wq, L0_gnn_bq, L0_gnn_Wk, L0_gnn_bk, L0_gnn_We, L0_gnn_be,
           L0_gnn_Wr, L0_gnn_br):
    import concourse.bacc as bacc
    from concourse.bass_utils import run_bass_kernel_spmd

    padded = GROUPS * GROUP
    x_rows = np.zeros((ROWS, D), np.float32)
    x_rows[:NODES] = x
    src_all = np.zeros((padded,), np.int32)
    src_all[:EDGES] = src
    dst_all = np.full((padded,), NO_NODE, np.int32)
    dst_all[:EDGES] = dst
    edge_all = np.zeros((padded, D), np.float32)
    edge_all[:EDGES] = edge_attr_256
    by_lane = lambda a: np.ascontiguousarray(a.reshape(GROUPS, TILES, LANES).transpose(2, 0, 1))
    arrays = {
        "x": x_rows,
        "dst_groups": dst_all.reshape(GROUPS, GROUP),
        "dst_lanes": by_lane(dst_all),
        "src_lanes": by_lane(src_all),
        "edges": np.ascontiguousarray(edge_all.reshape(GROUPS, GROUP, HALVES, LANES).transpose(0, 3, 2, 1)),
        "Wq": L0_gnn_Wq, "bq": L0_gnn_bq, "Wk": L0_gnn_Wk, "bk": L0_gnn_bk,
        "We": L0_gnn_We, "be": L0_gnn_be, "Wr": L0_gnn_Wr, "br": L0_gnn_br,
    }
    arrays = {f"in_{name}": np.ascontiguousarray(a) for name, a in arrays.items()}
    nc = bacc.Bacc("TRN2", target_bir_lowering=False, num_devices=1)
    args = [nc.dram_tensor(name, a.shape, mybir.dt.from_np(a.dtype), kind="ExternalInput").ap()
            for name, a in arrays.items()]
    out = nc.dram_tensor("out_rows", (ROWS, D), mybir.dt.float32, kind="ExternalOutput").ap()
    gnn_program(nc, *args, out)
    result = run_bass_kernel_spmd(nc, [arrays], core_ids=[0])
    return result.results[0]["out_rows"][:NODES]
```

```python
import numpy as np
import concourse.bass as bass
from concourse import mybir
from contextlib import ExitStack

LANES = 128
NODES = 6250
EDGES = 106250
D = 256
HALVES = D // LANES
BLOCKS = 52
ROWS = BLOCKS * LANES
TILES = 4
GROUP = TILES * LANES
GROUPS = -(-EDGES // GROUP)
UNROLL = 4
BODIES = GROUPS // UNROLL
CHUNKS = 2
GPART = GROUPS // CHUNKS
WIN = 48
PASSES = -(-NODES // WIN)
NO_NODE = -1
FAR = 1 << 20
EPS = 1e-5
XPARTS = 4
XPART = BLOCKS // XPARTS
NORM_STARTS = (0, BLOCKS // 4, BLOCKS // 2, BLOCKS)
NORM_PARTS = len(NORM_STARTS) - 1
NRING = 4
TURNS = BLOCKS // NRING
NORM_STEPS = (None, 0, 17)
STATS_STEPS = NORM_STEPS[2]
SIDE_TURNS = 6
PAIRS = NRING // 2
X_SLOTS = 8
OUT_SLOTS = 4
LOAD_TURNS = SIDE_TURNS + UNROLL
assert TURNS % OUT_SLOTS == 1 and UNROLL == OUT_SLOTS and NRING == TILES and X_SLOTS == UNROLL + 4
assert BLOCKS % NRING == 0 and BLOCKS % 2 == 0 and 2 * NRING * (TURNS - SIDE_TURNS) >= BLOCKS and BLOCKS % XPARTS == 0
assert GROUPS % UNROLL == 0 and GROUPS % CHUNKS == 0 and PASSES * WIN <= ROWS


def gnn_program(nc, x, dst_groups, dst_lanes, src_lanes, edges, Wq, bq, Wk, bk, We, be, Wr, br, out):
    F32, F32R = mybir.dt.float32, mybir.dt.float32r
    I32, I16 = mybir.dt.int32, mybir.dt.int16
    ALU, ACT, AX = mybir.AluOpType, mybir.ActivationFunctionType, mybir.AxisListType

    k_table = nc.dram_tensor("k_table", (ROWS, D), F32, kind="Internal").ap()
    q_table = nc.dram_tensor("q_table", (2, ROWS, D), F32R, kind="Internal").ap()
    rel_table = nc.dram_tensor("rel_table", (GROUPS, GROUP), I16, kind="Internal").ap()
    range_table = nc.dram_tensor("range_table", (2, GROUPS), F32, kind="Internal").ap()

    x_blocks = x.rearrange("(b p) d -> b p d", p=LANES)
    out_blocks = out.rearrange("(b p) d -> b p d", p=LANES)
    k_blocks = k_table.rearrange("(b p) d -> b p d", p=LANES)
    q_blocks = q_table.rearrange("s (b p) d -> s b p d", p=LANES)

    ctx = ExitStack()
    with ctx:
        def sb(name, shape, dt):
            return ctx.enter_context(nc.sbuf_tensor(name, shape, dt))

        def pb(name, shape):
            return ctx.enter_context(nc.psum_tensor(name, shape, F32))

        def sem(name):
            return ctx.enter_context(nc.semaphore(name))

        ident = sb("ident", [LANES, LANES], F32)
        window_cols = sb("window_cols", [LANES, PASSES * WIN], I16)
        lane_raw = sb("lane_raw", [2 * WIN, PASSES], F32)
        lane_wrap = sb("lane_wrap", [2 * WIN, 1], F32)
        lane_node = sb("lane_node", [2 * WIN, PASSES], F32)
        lane_id = sb("lane_id", [2 * WIN, 1], F32)
        src_idx = sb("src_idx", [LANES, GROUPS, TILES], I32)
        dst_idx = sb("dst_idx", [LANES, GROUPS, TILES], I32)
        rel_idx = sb("rel_idx", [LANES, GROUPS, TILES], F32)
        rel_g = sb("rel_g", [GPART, CHUNKS, GROUP], I16)
        top_g = sb("top_g", [GPART, CHUNKS], F32)
        low_g = sb("low_g", [GPART, CHUNKS], F32)
        win_g = sb("win_g", [GPART, CHUNKS], F32)
        ranges = sb("ranges", [LANES, 2, GROUPS], F32)
        spans = sb("spans", [LANES, GROUPS], F32)
        span = sb("span", [LANES, 1], F32)
        narrow = sb("narrow", [LANES, 1], F32)
        win_f = sb("win_f", [LANES, GROUPS], F32)
        win_tab = sb("win_tab", [LANES, GROUPS], I32)
        more_passes = sb("more_passes", [LANES, 1], I32)

        w_hi = sb("w_hi", [LANES, HALVES, 2 * D], F32R)
        w_lo = sb("w_lo", [LANES, HALVES, 2 * D], F32R)
        we_hi = sb("we_hi", [LANES, HALVES, D], F32R)
        we_lo = sb("we_lo", [LANES, HALVES, D], F32R)
        wr_hi = sb("wr_hi", [LANES, HALVES, D], F32R)
        wr_lo = sb("wr_lo", [LANES, HALVES, D], F32R)
        bias = sb("bias", [LANES, 2 * D], F32)
        bias_e = sb("bias_e", [LANES, D], F32)
        bias_r = sb("bias_r", [LANES, D], F32)

        stats = sb("stats", [LANES, BLOCKS, 6], F32)
        norm = sb("norm", [LANES, 6, BLOCKS], F32)
        mean2, diff, var, root, rstd, shift = (norm[:, i, :] for i in range(6))

        def norm_of(a, part):
            return a[:, NORM_STARTS[part]:NORM_STARTS[part + 1]]

        hn = sb("hn", [LANES, NRING, D], F32)
        hT_hi = sb("hT_hi", [LANES, NRING, D], F32R)
        hT_lo = sb("hT_lo", [LANES, NRING, D], F32R)

        ft = sb("ft", [LANES, HALVES, ROWS], F32)
        edge = sb("edge", [LANES, 4, HALVES, GROUP], F32)
        edge_hi = sb("edge_hi", [LANES, 2, HALVES, GROUP], F32R)
        edge_lo = sb("edge_lo", [LANES, 2, HALVES, GROUP], F32R)
        k_rows = sb("k_rows", [LANES, 4, TILES, D], F32)
        idx = sb("idx", [LANES, 4, TILES], I32)
        q_win = sb("q_win", [2 * WIN, 4, D], F32R)
        rel_row = sb("rel_row", [2 * WIN, 4, GROUP], I16)
        gap = sb("gap", [2 * WIN, GROUP], I16)
        pick = sb("pick", [2 * WIN, 2, GROUP], F32R)
        send = sb("send", [LANES, 2, TILES, LANES], F32R)
        pre = sb("pre", [LANES, 2, TILES * D], F32)
        m_hi = sb("m_hi", [LANES, 2, TILES * D], F32R)
        m_lo = sb("m_lo", [LANES, 2, TILES * D], F32R)
        x_all = ft[:].rearrange("p h r -> p (h r)").rearrange("p (b d) -> p b d", d=D)
        x_slots = [edge[:, u].rearrange("p h e -> p (h e)") for u in range(UNROLL)]
        slot_cols = 2 * NRING * D
        x_slots += [window_cols[:, u * slot_cols:(u + 1) * slot_cols].bitcast(F32) for u in range(3)]
        x_slots += [pre[:, 0, :]]
        x_slots = [slot.rearrange("p (b d) -> p b d", d=D) for slot in x_slots]
        result = k_rows
        kq = k_rows[:, 0:2].rearrange("p s t d -> p (s t d)").rearrange("p (b n) -> p b n", n=2 * D)
        q_parts = m_hi[:].rearrange("p s (b d) -> p b s d", d=D)
        dst_g = pre[0:GPART, 0, :].bitcast(I32).rearrange("p (c e) -> p c e", c=CHUNKS)
        dst_f = pre[0:GPART, 1, :].rearrange("p (c e) -> p c e", c=CHUNKS)
        w_raw = k_rows[:, 2].rearrange("p t d -> p (t d)").rearrange("p (h n) -> p h n", h=HALVES)
        we_raw = k_rows[:, 3, 0:HALVES]
        wr_raw = k_rows[:, 3, HALVES:2 * HALVES]
        sum_rows = sb("sum_rows", [LANES, 2, D], F32)

        p_edge = pb("p_edge", [LANES, 2, TILES * D])
        p_out = p_edge[:].rearrange("p s (v n) -> p s v n", v=PAIRS)
        p_sum = pb("p_sum", [LANES, 2, 512])
        p_turn = pb("p_turn", [LANES, 2, 512])

        s_dst = sem("dst_loaded")
        s_lanes = sem("lanes_loaded")
        s_wload = sem("node_weights_loaded")
        s_eload = sem("edge_weights_loaded")
        s_range = sem("range_stored")
        s_ranges = sem("ranges_loaded")
        s_rel = sem("rel_stored")
        s_prep = sem("prep_step")
        s_tab = sem("window_table_ready")
        s_wsplit = sem("node_weights_split")
        s_esplit = sem("edge_weights_split")
        s_zero = sem("zeroed")
        s_const = sem("constants_ready")
        s_x = [sem(f"x_loaded_{c}") for c in range(XPARTS)]
        s_norm = sem("layernorm_step")
        s_var = sem("variance_ready")
        s_root = sem("deviation_ready")
        s_inv = sem("reciprocal_ready")
        s_shift = sem("scale_and_shift_ready")
        s_stats = sem("row_statistics_ready")
        s_cleared = sem("ft_cleared")
        s_hn = sem("hn_ready")
        s_hT = sem("h_transposed")
        s_hhi = sem("hT_hi_ready")
        s_hlo = sem("hT_lo_ready")
        s_kqp = sem("kq_product_done")
        s_kq = sem("kq_ready")
        s_qhi = sem("q_hi_ready")
        s_qlo = sem("q_lo_ready")
        s_kstore = [sem(f"k_table_stored_{u}") for u in range(NRING)]
        s_qstore = [sem(f"q_table_stored_{u}") for u in range(NRING)]
        s_edge = [sem(f"edge_loaded_{u}") for u in range(UNROLL)]
        s_row = [sem(f"rel_row_loaded_{u}") for u in range(UNROLL)]
        s_win = [sem(f"q_window_loaded_{u}") for u in range(UNROLL)]
        s_rows = [sem(f"k_rows_gathered_{u}") for u in range(UNROLL)]
        s_go = sem("gathers_may_start")
        s_go_act = sem("scalar_may_go_on")
        s_idx = sem("idx_ready")
        s_ehi = sem("edge_hi_ready")
        s_elo = sem("edge_lo_ready")
        s_gap = sem("gap_ready")
        s_pick = sem("pick_ready")
        s_send = sem("send_ready")
        s_prod = sem("edge_product_done")
        s_pre = sem("pre_ready")
        s_mhi = sem("m_hi_ready")
        s_mlo = sem("m_lo_ready")
        s_sum = sem("sum_done")
        s_part = sem("part_ready")
        s_turn = sem("part_transposed")
        s_ft = sem("ft_added")
        s_xo = [sem(f"xo_loaded_{u}") for u in range(X_SLOTS)]
        s_fhi = sem("ft_hi_ready")
        s_flo = sem("ft_lo_ready")
        s_outp = sem("out_product_done")
        s_xbr = sem("x_plus_br_ready")
        s_fin = sem("out_ready")
        s_out = [sem(f"out_stored_{u}") for u in range(2)]
        s_free = sem("out_slot_free")

        def after(eng, semaphore, n):
            if isinstance(n, int) and n < 0:
                return
            eng.wait_ge(semaphore, n + 1)

        def stored(eng, stores, b, u):
            if isinstance(b, int) and b < NRING:
                return
            eng.wait_ge(stores[u], 16 // NRING * (b - u))

        def one(t, b):
            return t[:, bass.ds(b, 1), :].rearrange("p b d -> p (b d)")

        def visit(it, u):
            body, slot = it + u // UNROLL, u % UNROLL
            return body, slot, body * UNROLL + slot, body // BODIES, body % BODIES

        def window_start(eng, w, ps):
            return nc.s_assert_within(eng.snap(w + ps * WIN), 0, ROWS - WIN, skip_runtime_bounds_check_because=(
                "either there is one pass, or the window table is all zeros"))

        def passes_of(eng):
            eng.wait_ge(s_tab, 1)
            return eng.value_load(more_passes[0:1, 0:1], min_val=0, max_val=PASSES - 1) * BODIES + BODIES

        PREP_STEPS = 4 + 3 + 4 + CHUNKS + 2

        block = ctx.enter_context(nc.Block())

        @block.sync
        def _(sp):
            sp.dma_start(dst_g[:], dst_groups.rearrange("(p c) e -> p c e", c=CHUNKS)).then_inc(s_dst, 16)

            def load_x(c):
                blocks = slice(c * XPART, (c + 1) * XPART)
                sp.dma_start(x_all[:, blocks, :], x_blocks[blocks].rearrange("b p d -> p b d")).then_inc(s_x[c], 16)

            def load_weights(weights, biases, loaded):
                for w_ap, dst in weights:
                    sp.dma_start(dst, w_ap.rearrange("(h p) n -> p h n", p=LANES)).then_inc(loaded, 16)
                for b_ap, dst in biases:
                    sp.dma_start(dst, b_ap.rearrange("(a n) -> a n", a=1).to_broadcast([LANES, D]))\
                        .then_inc(loaded, 16)

            load_x(0)
            load_weights(((Wk, w_raw[:, :, 0:D]), (Wq, w_raw[:, :, D:2 * D])),
                         ((bk, bias[:, 0:D]), (bq, bias[:, D:2 * D]), (be, bias_e[:])), s_wload)
            sp.wait_ge(s_prep, 4)
            sp.dma_start(range_table[0].rearrange("(p c) -> p c", c=CHUNKS), low_g[:]).then_inc(s_range, 16)
            sp.dma_start(range_table[1].rearrange("(p c) -> p c", c=CHUNKS), top_g[:]).then_inc(s_range, 16)
            load_x(1)
            sp.wait_ge(s_range, 32)
            sp.dma_start(ranges[:], range_table.unsqueeze(0).to_broadcast([LANES, 2, GROUPS]))\
                .then_inc(s_ranges, 16)
            for c in range(2, XPARTS):
                load_x(c)

            def store_tables(b, u):
                after(sp, s_kq, b)
                sp.dma_start(k_blocks[bass.ds(b, 1)].rearrange("a p d -> (a p) d"), kq[:, u, 0:D])\
                    .then_inc(s_kstore[u], 16)
                after(sp, s_qhi, b)
                after(sp, s_qlo, b)
                sp.dma_start(q_blocks[:, bass.ds(b, 1)].rearrange("s a p d -> (a p) s d").bitcast(F32),
                             q_parts[:, u].bitcast(F32)).then_inc(s_qstore[u], 16)

            def load_edge(it, u):
                body, slot, n, _, gb = visit(it, u)
                after(sp, s_ehi, n - 4)
                after(sp, s_elo, n - 4)
                g = gb * UNROLL + slot
                src = edges[g] if isinstance(g, int) else edges[bass.ds(g, 1)].rearrange("a p h e -> (a p) h e")
                sp.dma_start(edge[:, slot], src).then_inc(s_edge[slot], 16)

            for t in range(LOAD_TURNS):
                for u in range(NRING):
                    store_tables(NRING * t + u, u)
                if t == 1:
                    load_weights(((We, we_raw[:]), (Wr, wr_raw[:])), ((br, bias_r[:]),), s_eload)
                if t == 2:
                    sp.dma_start(dst_idx[:], dst_lanes).then_inc(s_lanes, 16)
                if t == 3:
                    sp.dma_start(src_idx[:], src_lanes).then_inc(s_lanes, 16)
                if t == SIDE_TURNS - 1:
                    sp.wait_ge(s_prep, PREP_STEPS - 2)
                    sp.dma_start(rel_table.rearrange("(p c) e -> p c e", c=CHUNKS), rel_g[:]).then_inc(s_rel, 16)
                if t >= SIDE_TURNS:
                    load_edge(0, t - SIDE_TURNS)
            with sp.Fori(LOAD_TURNS, TURNS) as it:
                for u in range(NRING):
                    store_tables(NRING * it + u, u)

            def load_row(it, u):
                body, slot, n, _, gb = visit(it, u)
                after(sp, s_pick, n - 4)
                g = gb * UNROLL + slot
                sp.dma_start(rel_row[:, slot, :], rel_table[bass.ds(g, 1), :].to_broadcast([2 * WIN, GROUP]))\
                    .then_inc(s_row[slot], 16)

            def load_window(it, u):
                body, slot, n, ps, gb = visit(it, u)
                g = gb * UNROLL + slot
                w = sp.value_load(win_tab[0:1, bass.ds(g, 1)], min_val=0, max_val=NODES - WIN)
                w0 = window_start(sp, w, ps)
                after(sp, s_prod, n - 4)
                for s in range(2):
                    sp.dma_start(q_win[s * WIN:(s + 1) * WIN, slot, :].bitcast(F32),
                                 q_table[s, bass.ds(w0, WIN), :].bitcast(F32)).then_inc(s_win[slot], 16)

            sp.wait_ge(s_rel, 16)
            for u in range(UNROLL):
                load_row(0, u)
            bodies = passes_of(sp)
            for u in range(NRING):
                sp.wait_ge(s_qstore[u], 16 * TURNS)
            for u in range(UNROLL):
                load_window(0, u)
            with sp.Fori(1, bodies) as it:
                for u in range(UNROLL):
                    load_edge(it, u)
                    load_row(it, u)
                    load_window(it, u)

            def load_xo(t):
                x_turn = x_blocks[NRING * t:NRING * (t + 1)].rearrange("b p d -> p b d")
                sp.dma_start(x_slots[t % X_SLOTS], x_turn)\
                    .then_inc(s_xo[t % X_SLOTS], 16)

            for t in range(UNROLL):
                sp.wait_ge(s_ehi, bodies * UNROLL - (UNROLL - 1) + t)
                sp.wait_ge(s_elo, bodies * UNROLL - (UNROLL - 1) + t)
                load_xo(t)
            sp.wait_ge(s_send, bodies * UNROLL)
            for t in range(UNROLL, X_SLOTS - 1):
                load_xo(t)
            sp.wait_ge(s_mhi, bodies * UNROLL - 1)
            sp.wait_ge(s_mlo, bodies * UNROLL - 1)
            load_xo(X_SLOTS - 1)
            for t in range(TURNS):
                after(sp, s_fin, PAIRS * (t + 1) - 1)
                sp.dma_start(out_blocks[NRING * t:NRING * (t + 1)].rearrange("b p d -> p b d"),
                             result[:, t % OUT_SLOTS]).then_inc(s_out[t % 2], 16)
                if t + X_SLOTS < TURNS:
                    after(sp, s_xbr, t)
                    load_xo(t + X_SLOTS)
                if t > 0:
                    sp.wait_ge(s_out[(t - 1) % 2], 16 * ((t - 1) // 2 + 1))
                    sp.sem_inc(s_free, 1)
            sp.wait_ge(s_out[(TURNS - 1) % 2], 16 * ((TURNS - 1) // 2 + 1))

        @block.gpsimd
        def _(pool):
            linked = [0]

            def link(ins):
                linked[0] += 1
                ins.then_inc(s_norm, 1)
                pool.wait_ge(s_norm, linked[0])

            nc.gpsimd.memset(ident[:], 0.0).then_inc(s_zero, 1)
            nc.gpsimd.iota(lane_raw[:], pattern=[[WIN, PASSES]], base=0, channel_multiplier=1,
                           allow_small_or_imprecise_dtypes=True).then_inc(s_const, 1)
            nc.gpsimd.iota(lane_id[:], pattern=[[0, 1]], base=0, channel_multiplier=1,
                           allow_small_or_imprecise_dtypes=True).then_inc(s_const, 1)
            pool.wait_ge(s_zero, 1)
            nc.gpsimd.affine_select(out=ident[:], in_=ident[:], compare_op=ALU.not_equal, fill=1.0, base=0,
                                    pattern=[[-1, LANES]], channel_multiplier=1).then_inc(s_const, 1)
            nc.gpsimd.iota(window_cols[:], pattern=[[1, PASSES * WIN]], base=0, channel_multiplier=0,
                           allow_small_or_imprecise_dtypes=True).then_inc(s_const, 1)
            nc.gpsimd.memset(send[:].bitcast(F32), 0.0).then_inc(s_const, 1)

            def variance(part):
                blocks = slice(NORM_STARTS[part], NORM_STARTS[part + 1])
                m, d, v = (norm_of(a, part) for a in (mean2, diff, var))
                pool.wait_ge(s_stats, NORM_STARTS[part + 1])
                link(nc.gpsimd.tensor_tensor(m, stats[:, blocks, 1], stats[:, blocks, 4], ALU.add))
                link(nc.gpsimd.tensor_tensor(d, stats[:, blocks, 1], stats[:, blocks, 4], ALU.subtract))
                link(nc.gpsimd.tensor_tensor(d, d, d, ALU.mult))
                link(nc.gpsimd.tensor_scalar(d, d, D / 4.0, None, ALU.mult))
                link(nc.gpsimd.tensor_tensor(v, stats[:, blocks, 2], stats[:, blocks, 5], ALU.add))
                link(nc.gpsimd.tensor_tensor(v, d, v, ALU.add))
                nc.gpsimd.tensor_scalar(v, v, 1.0 / D, EPS, ALU.mult, ALU.add).then_inc(s_var, 1)

            def scale_and_shift(part):
                m, d, v, r, t = (norm_of(a, part) for a in (mean2, diff, var, rstd, shift))
                pool.wait_ge(s_inv, part + 1)
                link(nc.gpsimd.tensor_tensor(d, r, r, ALU.mult))
                link(nc.gpsimd.tensor_tensor(d, d, v, ALU.mult))
                link(nc.gpsimd.tensor_scalar(d, d, -0.5, 1.5, ALU.mult, ALU.add))
                link(nc.gpsimd.tensor_tensor(r, r, d, ALU.mult))
                link(nc.gpsimd.tensor_tensor(t, m, r, ALU.mult))
                nc.gpsimd.tensor_scalar(t, t, -0.5, None, ALU.mult).then_inc(s_shift, 1)

            def make_q_lo(b, u):
                after(pool, s_qhi, b)
                stored(pool, s_qstore, b, u)
                nc.gpsimd.tensor_tensor(q_parts[:, u, 1], kq[:, u, D:2 * D], q_parts[:, u, 0].bitcast(F32),
                                        ALU.subtract).then_inc(s_qlo, 1)

            variance(0)
            scale_and_shift(0)
            for b in range(NRING * SIDE_TURNS):
                for part in range(1, NORM_PARTS):
                    if b == NORM_STEPS[part]:
                        variance(part)
                    if b == NORM_STEPS[part] + 3:
                        scale_and_shift(part)
                make_q_lo(b, b % NRING)
            with pool.Fori(SIDE_TURNS, TURNS) as it:
                for u in range(NRING):
                    make_q_lo(NRING * it + u, u)

            bodies = passes_of(pool)
            pool.wait_ge(s_qlo, BLOCKS)
            for u in range(NRING):
                pool.wait_ge(s_kstore[u], 16 * TURNS)

            def gather(it, u):
                _, slot, n, _, _ = visit(it, u)
                after(pool, s_idx, n)
                after(pool, s_pre, n - 4)
                pool.sem_inc(s_go, 1)
                for j in range(TILES):
                    nc.gpsimd.indirect_dma_start(
                        out=k_rows[:, slot, j, :], out_offset=None, in_=k_table,
                        in_offset=bass.IndirectOffsetOnAxis(ap=idx[:, slot, j:j + 1], axis=0),
                    ).then_inc(s_rows[slot], 16)

            for u in range(UNROLL):
                gather(0, u)
            with pool.Fori(1, bodies) as it:
                for u in range(UNROLL):
                    gather(it, u)

            pool.wait_ge(s_pre, bodies * UNROLL)
            for t in range(TURNS):
                pool.wait_ge(s_xo[t % X_SLOTS], 16 * (t // X_SLOTS + 1))
                after(pool, s_free, t - OUT_SLOTS)
                nc.gpsimd.tensor_tensor(result[:, t % OUT_SLOTS], x_slots[t % X_SLOTS],
                                        bias_r[:].unsqueeze(1).to_broadcast([LANES, NRING, D]),
                                        ALU.add).then_inc(s_xbr, 1)

        @block.scalar
        def _(act):
            def deviation(part):
                act.wait_ge(s_var, part + 1)
                nc.scalar.activation(norm_of(root, part), norm_of(var, part), ACT.Sqrt).then_inc(s_root, 1)

            deviation(0)
            act.wait_ge(s_wload, 16 * 5)
            nc.scalar.activation(w_hi[:], w_raw[:], ACT.Copy).then_inc(s_wsplit, 1)
            act.wait_ge(s_shift, 1)

            def make_h(b, u):
                after(act, s_hT, b - NRING)
                act.sem_inc(s_go_act, 1)
                nc.scalar.activation(hn[:, u, :], one(x_all, b), ACT.Relu,
                                     bias=shift[:, bass.ds(b, 1)], scale=rstd[:, bass.ds(b, 1)]).then_inc(s_hn, 1)

            def h_hi(b, u):
                after(act, s_hT, b)
                after(act, s_kqp, b - NRING)
                nc.scalar.activation(hT_hi[:, u, :], p_turn[:, u % 2, 0:D], ACT.Copy).then_inc(s_hhi, 1)

            def round_q(b, u):
                after(act, s_kq, b)
                stored(act, s_qstore, b, u)
                nc.scalar.activation(q_parts[:, u, 0], kq[:, u, D:2 * D], ACT.Copy).then_inc(s_qhi, 1)

            def node_step(t, u, first=False, last=False):
                b = NRING * t + u
                if isinstance(b, int) and b + 3 in NORM_STARTS[:-1]:
                    act.wait_ge(s_shift, NORM_STARTS.index(b + 3) + 1)
                if not (last and u + 3 >= NRING):
                    make_h(b + 3, (u + 3) % NRING)
                if not (last and u + 1 >= NRING):
                    h_hi(b + 1, (u + 1) % NRING)
                if not (first and u < 1):
                    round_q(b - 1, (u - 1) % NRING)

            for u in range(3):
                make_h(u, u)
            h_hi(0, 0)
            for b in range(NRING * SIDE_TURNS):
                node_step(b // NRING, b % NRING, first=b < NRING)
                for part in range(1, NORM_PARTS):
                    if b == NORM_STEPS[part] + 1:
                        deviation(part)
                if b == NORM_STARTS[1]:
                    act.wait_ge(s_eload, 16 * 3)
                    nc.scalar.activation(we_hi[:], we_raw[:], ACT.Copy).then_inc(s_esplit, 1)
                    nc.scalar.activation(wr_hi[:], wr_raw[:], ACT.Copy).then_inc(s_esplit, 1)
            with act.Fori(SIDE_TURNS, TURNS - 1) as it:
                for u in range(NRING):
                    node_step(it, u)
            for u in range(NRING):
                node_step(TURNS - 1, u, last=True)
            round_q(BLOCKS - 1, NRING - 1)

            def copy_idx(it, u):
                _, slot, n, _, gb = visit(it, u)
                after(act, s_pre, n - 4)
                nc.scalar.copy(idx[:, slot, :], src_idx[:, bass.ds(gb * UNROLL + slot, 1), :]
                               .rearrange("p a t -> p (a t)")).then_inc(s_idx, 1)

            def edge_high(it, u):
                body, slot, n, _, _ = visit(it, u)
                act.wait_ge(s_edge[slot], 16 * (body + 1))
                after(act, s_prod, n - 2)
                nc.scalar.activation(edge_hi[:, slot % 2], edge[:, slot], ACT.Copy).then_inc(s_ehi, 1)

            def make_pick(it, u):
                body, slot, n, ps, _ = visit(it, u)
                act.wait_ge(s_row[slot], 16 * (body + 1))
                after(act, s_prod, n - 2)
                after(act, s_pick, n - 1)
                act.sem_inc(s_go_act, 1)
                nc.scalar.activation(gap[:], rel_row[:, slot, :], ACT.Abs, scale=-1.0,
                                     bias=lane_node[:, bass.ds(ps, 1)]).then_inc(s_gap, 1)
                after(act, s_gap, n)
                nc.scalar.activation(pick[:, slot % 2, :], gap[:], ACT.Relu, bias=1.0, scale=-1.0)\
                    .then_inc(s_pick, 1)

            def message_high(it, u):
                _, slot, n, _, _ = visit(it, u)
                after(act, s_pre, n)
                after(act, s_sum, n - 2)
                nc.scalar.activation(m_hi[:, slot % 2, :], pre[:, slot % 2, :], ACT.Relu).then_inc(s_mhi, 1)

            def take_sum(it, u):
                _, slot, n, _, _ = visit(it, u)
                after(act, s_sum, n)
                after(act, s_turn, n - 2)
                nc.scalar.activation(sum_rows[:, slot % 2, :], p_sum[:, slot % 2, 0:D], ACT.Copy)\
                    .then_inc(s_part, 1)

            def steps(it, first=False, last=False):
                for u in range(UNROLL):
                    if not (last and u + 3 >= UNROLL):
                        copy_idx(it, u + 3)
                    if not (last and u + 2 >= UNROLL):
                        edge_high(it, u + 2)
                    message_high(it, u)
                    if not (last and u + 2 >= UNROLL):
                        make_pick(it, u + 2)
                    if not (first and u < 2):
                        take_sum(it, u - 2)

            act.wait_ge(s_lanes, 32)
            for u in range(3):
                copy_idx(0, u)
            for u in range(2):
                edge_high(0, u)
            bodies = passes_of(act)
            for u in range(2):
                make_pick(0, u)
            steps(0, first=True)
            with act.Fori(1, bodies - 1) as it:
                steps(it)
            steps(bodies - 1, last=True)
            take_sum(bodies - 1, UNROLL - 2)
            take_sum(bodies - 1, UNROLL - 1)

            def ft_high(b, u):
                after(act, s_outp, b - NRING)
                act.sem_inc(s_go_act, 1)
                nc.scalar.activation(hT_hi[:, u, :].rearrange("p (h n) -> p h n", h=HALVES),
                                     ft[:, :, bass.ds(b * LANES, LANES)], ACT.Copy).then_inc(s_fhi, 1)

            act.wait_ge(s_ft, bodies * UNROLL)
            for u in range(NRING):
                ft_high(u, u)
            with act.Fori(1, TURNS) as it:
                for u in range(NRING):
                    ft_high(NRING * it + u, u)

        @block.vector
        def _(dve):
            linked = [0]

            def link(ins):
                linked[0] += 1
                ins.then_inc(s_prep, 1)
                dve.wait_ge(s_prep, linked[0])

            dve.wait_ge(s_dst, 16)
            link(nc.vector.tensor_reduce(top_g[:], dst_g[:], axis=AX.X, op=ALU.max))
            link(nc.vector.tensor_scalar(dst_f[:], dst_g[:], 0.0, float(FAR), ALU.is_lt, ALU.mult))
            link(nc.vector.tensor_tensor(dst_f[:], dst_f[:], dst_g[:], ALU.add))
            link(nc.vector.tensor_reduce(low_g[:], dst_f[:], axis=AX.X, op=ALU.min))

            def row_statistics(b):
                if b % XPART == 0:
                    dve.wait_ge(s_x[b // XPART], 16)
                nc.vector.bn_stats(stats[:, b, :], x_all[:, b, :]).then_inc(s_stats, 1)

            def inverse(part):
                dve.wait_ge(s_root, part + 1)
                nc.vector.reciprocal(norm_of(rstd, part), norm_of(root, part)).then_inc(s_inv, 1)

            for b in range(NORM_STARTS[1]):
                row_statistics(b)
            dve.wait_ge(s_wload, 16 * 5)
            nc.vector.tensor_tensor(bias[:, D:2 * D], bias[:, D:2 * D], bias_e[:], ALU.add).then_inc(s_wsplit, 1)
            inverse(0)
            dve.wait_ge(s_wsplit, 2)
            nc.vector.tensor_tensor(w_lo[:], w_raw[:], w_hi[:].bitcast(F32), ALU.subtract).then_inc(s_wsplit, 1)
            dve.wait_ge(s_wsplit, 3)

            def h_lo(b, u):
                after(dve, s_hhi, b)
                after(dve, s_kqp, b - NRING)
                nc.vector.tensor_tensor(hT_lo[:, u, :], p_turn[:, u % 2, 0:D], hT_hi[:, u, :].bitcast(F32),
                                        ALU.subtract).then_inc(s_hlo, 1)

            def add_bias(b, u):
                after(dve, s_kqp, b)
                stored(dve, s_kstore, b, u)
                after(dve, s_qlo, b - NRING)
                nc.vector.tensor_tensor(kq[:, u, :], p_sum[:, u % 2, :], bias[:], ALU.add).then_inc(s_kq, 1)

            def node_step(t, u, last=False):
                if not (last and u + 1 >= NRING):
                    h_lo(NRING * t + u + 1, (u + 1) % NRING)
                pair = NRING * (t - SIDE_TURNS) + u
                if not (last and pair >= BLOCKS // 2):
                    clear(pair)
                add_bias(NRING * t + u, u)

            def clear(pair):
                after(dve, s_hn, 2 * pair + 1)
                zeros = send[:, 0, 0:2, :].bitcast(F32).rearrange("p t n -> p (t n)").unsqueeze(1)\
                    .to_broadcast([LANES, 2, D])
                nc.vector.tensor_copy(x_all[:, bass.ds(2 * pair, 2), :], zeros).then_inc(s_cleared, 1)

            def widest_span():
                dve.wait_ge(s_ranges, 16)
                link(nc.vector.tensor_tensor(spans[:], ranges[:, 1, :], ranges[:, 0, :], ALU.subtract))
                link(nc.vector.tensor_reduce(span[:], spans[:], axis=AX.X, op=ALU.max))
                link(nc.vector.tensor_scalar(narrow[:], span[:], float(WIN - 1), None, ALU.is_le))

            def window_starts():
                nc.vector.tensor_scalar(win_f[:], ranges[:, 0, :], float(NODES - WIN), narrow[:],
                                        ALU.min, ALU.mult).then_inc(s_prep, 1)
                nc.vector.tensor_scalar(win_g[:], low_g[:], float(NODES - WIN), narrow[0:GPART, :],
                                        ALU.min, ALU.mult).then_inc(s_prep, 1)
                nc.vector.tensor_scalar(more_passes[:], narrow[:], float(1 - PASSES), float(PASSES - 1),
                                        ALU.mult, ALU.add).then_inc(s_prep, 1)
                nc.vector.tensor_scalar(lane_wrap[:], lane_id[:], float(WIN), float(WIN), ALU.is_ge, ALU.mult)\
                    .then_inc(s_prep, 1)

            def group_nodes(c):
                dve.wait_ge(s_prep, 4 + 3 + 4)
                nc.vector.tensor_scalar(rel_g[:, c, :], dst_g[:, c, :], win_g[:, c:c + 1], None,
                                        ALU.subtract).then_inc(s_prep, 1)

            def window_table():
                nc.vector.tensor_copy(win_tab[:], win_f[:]).then_inc(s_prep, 1)
                nc.vector.tensor_scalar(lane_node[:], lane_raw[:], lane_wrap[:], None, ALU.subtract)\
                    .then_inc(s_prep, 1)
                dve.wait_ge(s_prep, PREP_STEPS)
                dve.sem_inc(s_tab, 1)

            def edge_weights_low():
                dve.wait_ge(s_esplit, 2)
                nc.vector.tensor_tensor(we_lo[:], we_raw[:], we_hi[:].bitcast(F32), ALU.subtract)\
                    .then_inc(s_esplit, 1)
                nc.vector.tensor_tensor(wr_lo[:], wr_raw[:], wr_hi[:].bitcast(F32), ALU.subtract)\
                    .then_inc(s_esplit, 1)

            dve.wait_ge(s_const, 5)
            h_lo(0, 0)
            for b in range(NORM_STARTS[1], NORM_STARTS[2]):
                if b == NORM_STARTS[1] + 4:
                    h_lo(1, 1)
                row_statistics(b)
            ready = NORM_STARTS[2]
            for b in range(NRING * SIDE_TURNS):
                if b > 0:
                    h_lo(b + 1, (b + 1) % NRING)
                for n in range(ready, BLOCKS):
                    if (n - ready) * STATS_STEPS // (BLOCKS - ready) == b:
                        row_statistics(n)
                add_bias(b, b % NRING)
                for part in range(1, NORM_PARTS):
                    if b == NORM_STEPS[part] + 2:
                        inverse(part)
                if b == NORM_STARTS[1] + 4:
                    widest_span()
                if b == NORM_STARTS[1] + 5:
                    window_starts()
                if b == NORM_STARTS[1] + 6:
                    group_nodes(0)
                if b == NORM_STARTS[1] + 7:
                    group_nodes(1)
                if b == NORM_STARTS[1] + 8:
                    window_table()
                if b == NORM_STARTS[1] + 9:
                    edge_weights_low()
            with dve.Fori(SIDE_TURNS, TURNS - 1) as it:
                for u in range(NRING):
                    node_step(it, u)
            for u in range(NRING):
                node_step(TURNS - 1, u, last=True)

            def edge_low(it, u):
                body, slot, n, _, _ = visit(it, u)
                after(dve, s_ehi, n)
                after(dve, s_prod, n - 2)
                nc.vector.tensor_tensor(edge_lo[:, slot % 2], edge[:, slot], edge_hi[:, slot % 2].bitcast(F32),
                                        ALU.subtract).then_inc(s_elo, 1)

            def make_send(it, u):
                body, slot, n, ps, gb = visit(it, u)
                after(dve, s_sum, n - 2)
                rel = rel_idx[:, bass.ds(gb * UNROLL + slot, 1), :].rearrange("p a t -> p (a t)")
                nc.vector.tensor_tensor(
                    send[:, slot % 2, :, 0:WIN], rel.unsqueeze(2).to_broadcast([LANES, TILES, WIN]),
                    window_cols[:, bass.ds(ps * WIN, WIN)].unsqueeze(1).to_broadcast([LANES, TILES, WIN]),
                    ALU.is_equal).then_inc(s_send, 1)

            def add_rows(it, u):
                body, slot, n, _, _ = visit(it, u)
                after(dve, s_prod, n)
                dve.wait_ge(s_rows[slot], 16 * TILES * (body + 1))
                after(dve, s_mlo, n - 2)
                nc.vector.tensor_tensor(pre[:, slot % 2, :], p_edge[:, slot % 2, :],
                                        k_rows[:, slot].rearrange("p t d -> p (t d)"), ALU.add).then_inc(s_pre, 1)

            def message_low(it, u):
                _, slot, n, _, _ = visit(it, u)
                after(dve, s_mhi, n)
                after(dve, s_sum, n - 2)
                nc.vector.scalar_tensor_tensor(m_lo[:, slot % 2, :], pre[:, slot % 2, :], 0.0,
                                               m_hi[:, slot % 2, :].bitcast(F32), ALU.max, ALU.subtract)\
                    .then_inc(s_mlo, 1)

            def add_sum(it, u):
                _, slot, n, ps, gb = visit(it, u)
                w = dve.value_load(win_tab[0:1, bass.ds(gb * UNROLL + slot, 1)], min_val=0, max_val=NODES - WIN)
                w0 = window_start(dve, w, ps)
                after(dve, s_turn, n)
                after(dve, s_ft, n - 1)
                window = ft[:, :, bass.ds(w0, WIN)]
                turned = p_turn[:, slot % 2, 0:D].rearrange("p (h n) -> p h n", h=HALVES)[:, :, 0:WIN]
                nc.vector.tensor_tensor(window, window, turned, ALU.add).then_inc(s_ft, 1)

            def steps(it, first=False, last=False):
                for u in range(UNROLL):
                    add_rows(it, u)
                    if not (last and u + 2 >= UNROLL):
                        edge_low(it, u + 2)
                    make_send(it, u)
                    message_low(it, u)
                    if not (first and u < 3):
                        add_sum(it, u - 3)

            dve.wait_ge(s_lanes, 32)
            nc.vector.tensor_tensor(rel_idx[:], dst_idx[:], win_f[:].unsqueeze(2).to_broadcast(
                [LANES, GROUPS, TILES]), ALU.subtract).then_inc(s_prep, 1)
            dve.wait_ge(s_prep, PREP_STEPS + 1)
            for u in range(2):
                edge_low(0, u)
            dve.wait_ge(s_cleared, BLOCKS // 2)
            bodies = passes_of(dve)
            steps(0, first=True)
            with dve.Fori(1, bodies - 1) as it:
                steps(it)
            steps(bodies - 1, last=True)
            for u in range(UNROLL - 3, UNROLL):
                add_sum(bodies - 1, u)

            def ft_low(b, u):
                after(dve, s_fhi, b)
                after(dve, s_outp, b - NRING)
                nc.vector.tensor_tensor(hT_lo[:, u, :].rearrange("p (h n) -> p h n", h=HALVES),
                                        ft[:, :, bass.ds(b * LANES, LANES)],
                                        hT_hi[:, u, :].bitcast(F32).rearrange("p (h n) -> p h n", h=HALVES),
                                        ALU.subtract).then_inc(s_flo, 1)

            def finish(it, j, v):
                t = OUT_SLOTS * it + j
                after(dve, s_outp, NRING * t + 2 * v + 1)
                after(dve, s_xbr, t)
                pair = result[:, j, 2 * v:2 * v + 2, :]
                nc.vector.tensor_tensor(pair, p_out[:, j % 2, v].rearrange("p (b d) -> p b d", d=D), pair,
                                        ALU.add).then_inc(s_fin, 1)

            def out_turn(it, j, last=False):
                for u in range(NRING):
                    if not (last and u + 3 >= NRING):
                        ft_low(NRING * (OUT_SLOTS * it + j) + u + 3, (u + 3) % NRING)
                    if u % 2:
                        finish(it, j, u // 2)

            for u in range(3):
                ft_low(u, u)
            for j in range(OUT_SLOTS):
                out_turn(0, j)
            with dve.Fori(1, TURNS // OUT_SLOTS) as it:
                for j in range(OUT_SLOTS):
                    out_turn(it, j)
            out_turn(TURNS // OUT_SLOTS, 0, last=True)

        @block.tensor
        def _(pe):
            def split_product(target, a_hi, a_lo, b_hi, b_lo, stop=True):
                for h in range(HALVES):
                    for n, (a, b) in enumerate(((a_hi, b_hi), (a_hi, b_lo), (a_lo, b_hi))):
                        ins = nc.tensor.matmul(target, a(h), b[:, h, :], start=(h == 0 and n == 0),
                                               stop=(stop and h == HALVES - 1 and n == 2))
                return ins

            def turn_h(b, u):
                after(pe, s_hn, b)
                after(pe, s_hlo, b - 2)
                for h in range(HALVES):
                    ins = nc.tensor.transpose(p_turn[:, u % 2, h * LANES:(h + 1) * LANES],
                                              hn[:, u, h * LANES:(h + 1) * LANES], ident[:])
                ins.then_inc(s_hT, 1)

            def node_product(b, u):
                after(pe, s_hhi, b)
                after(pe, s_hlo, b)
                after(pe, s_kq, b - 2)
                split_product(p_sum[:, u % 2, :], lambda h: hT_hi[:, u, h * LANES:(h + 1) * LANES],
                              lambda h: hT_lo[:, u, h * LANES:(h + 1) * LANES], w_hi, w_lo).then_inc(s_kqp, 1)

            pe.wait_ge(s_const, 3)
            def node_step(t, u, last=False):
                if not (last and u + 2 >= NRING):
                    turn_h(NRING * t + u + 2, (u + 2) % NRING)
                node_product(NRING * t + u, u)

            turn_h(0, 0)
            turn_h(1, 1)
            pe.wait_ge(s_wsplit, 3)
            for u in range(NRING):
                node_step(0, u)
            with pe.Fori(1, TURNS - 1) as it:
                for u in range(NRING):
                    node_step(it, u)
            for u in range(NRING):
                node_step(TURNS - 1, u, last=True)

            def edge_product(it, u):
                body, slot, n, _, _ = visit(it, u)
                after(pe, s_ehi, n)
                after(pe, s_elo, n)
                after(pe, s_pick, n)
                pe.wait_ge(s_win[slot], 32 * (body + 1))
                after(pe, s_pre, n - 2)
                for j in range(TILES):
                    target = p_edge[:, slot % 2, j * D:(j + 1) * D]
                    tile = slice(j * LANES, (j + 1) * LANES)
                    split_product(target, lambda h: edge_hi[:, slot % 2, h, tile],
                                  lambda h: edge_lo[:, slot % 2, h, tile], we_hi, we_lo, stop=False)
                    ins = nc.tensor.matmul(target, pick[:, slot % 2, tile], q_win[:, slot, :],
                                           start=False, stop=True)
                ins.then_inc(s_prod, 1)

            def turn_part(it, u):
                _, slot, n, _, _ = visit(it, u)
                after(pe, s_part, n)
                after(pe, s_ft, n - 2)
                for h in range(HALVES):
                    ins = nc.tensor.transpose(p_turn[:, slot % 2, h * LANES:(h + 1) * LANES],
                                              sum_rows[:, slot % 2, h * LANES:(h + 1) * LANES], ident[:])
                ins.then_inc(s_turn, 1)

            def window_sum(it, u):
                _, slot, n, _, _ = visit(it, u)
                after(pe, s_send, n)
                after(pe, s_mhi, n)
                after(pe, s_mlo, n)
                after(pe, s_part, n - 2)
                for j in range(TILES):
                    for m in (m_hi, m_lo):
                        ins = nc.tensor.matmul(p_sum[:, slot % 2, 0:D], send[:, slot % 2, j, :],
                                               m[:, slot % 2, j * D:(j + 1) * D],
                                               start=(j == 0 and m is m_hi), stop=(j == TILES - 1 and m is m_lo))
                ins.then_inc(s_sum, 1)

            def steps(it, first=False, last=False):
                for u in range(UNROLL):
                    if not (last and u + 1 >= UNROLL):
                        edge_product(it, u + 1)
                    if not (first and u < 1):
                        window_sum(it, u - 1)
                    if not (first and u < 2):
                        turn_part(it, u - 2)

            bodies = passes_of(pe)
            pe.wait_ge(s_esplit, 4)
            edge_product(0, 0)
            steps(0, first=True)
            with pe.Fori(1, bodies - 1) as it:
                steps(it)
            steps(bodies - 1, last=True)
            turn_part(bodies - 1, UNROLL - 2)
            window_sum(bodies - 1, UNROLL - 1)
            turn_part(bodies - 1, UNROLL - 1)

            def out_turn(it, j):
                t = OUT_SLOTS * it + j
                for u in range(NRING):
                    b = NRING * t + u
                    after(pe, s_fhi, b)
                    after(pe, s_flo, b)
                    if u % 2 == 0:
                        after(pe, s_fin, PAIRS * (t - 2) + u // 2)
                    split_product(p_out[:, j % 2, u // 2, (u % 2) * D:(u % 2 + 1) * D],
                                  lambda h: hT_hi[:, u, h * LANES:(h + 1) * LANES],
                                  lambda h: hT_lo[:, u, h * LANES:(h + 1) * LANES], wr_hi, wr_lo).then_inc(s_outp, 1)

            for j in range(OUT_SLOTS):
                out_turn(0, j)
            with pe.Fori(1, TURNS // OUT_SLOTS) as it:
                for j in range(OUT_SLOTS):
                    out_turn(it, j)
            out_turn(TURNS // OUT_SLOTS, 0)


def kernel(x, src, dst, edge_attr_256, L0_gnn_Wq, L0_gnn_bq, L0_gnn_Wk, L0_gnn_bk, L0_gnn_We, L0_gnn_be,
           L0_gnn_Wr, L0_gnn_br):
    import concourse.bacc as bacc
    from concourse.bass_utils import run_bass_kernel_spmd

    padded = GROUPS * GROUP
    x_rows = np.zeros((ROWS, D), np.float32)
    x_rows[:NODES] = x
    src_all = np.zeros((padded,), np.int32)
    src_all[:EDGES] = src
    dst_all = np.full((padded,), NO_NODE, np.int32)
    dst_all[:EDGES] = dst
    edge_all = np.zeros((padded, D), np.float32)
    edge_all[:EDGES] = edge_attr_256
    by_lane = lambda a: np.ascontiguousarray(a.reshape(GROUPS, TILES, LANES).transpose(2, 0, 1))
    arrays = {
        "x": x_rows,
        "dst_groups": dst_all.reshape(GROUPS, GROUP),
        "dst_lanes": by_lane(dst_all),
        "src_lanes": by_lane(src_all),
        "edges": np.ascontiguousarray(edge_all.reshape(GROUPS, GROUP, HALVES, LANES).transpose(0, 3, 2, 1)),
        "Wq": L0_gnn_Wq, "bq": L0_gnn_bq, "Wk": L0_gnn_Wk, "bk": L0_gnn_bk,
        "We": L0_gnn_We, "be": L0_gnn_be, "Wr": L0_gnn_Wr, "br": L0_gnn_br,
    }
    arrays = {f"in_{name}": np.ascontiguousarray(a) for name, a in arrays.items()}
    nc = bacc.Bacc("TRN2", target_bir_lowering=False, num_devices=1)
    args = [nc.dram_tensor(name, a.shape, mybir.dt.from_np(a.dtype), kind="ExternalInput").ap()
            for name, a in arrays.items()]
    out = nc.dram_tensor("out_rows", (ROWS, D), mybir.dt.float32, kind="ExternalOutput").ap()
    gnn_program(nc, *args, out)
    result = run_bass_kernel_spmd(nc, [arrays], core_ids=[0])
    return result.results[0]["out_rows"][:NODES]
```
